# Optimizing a Trainium2 kernel written in Bass

```python
import numpy as np
import jax
import jax.numpy as jnp

def _softmax(x, axis=-1):
    return jax.nn.softmax(x, axis=axis)

def _gelu(x):
    return jax.nn.gelu(x, approximate=True)

def _silu(x):
    return jax.nn.silu(x)

def _sigmoid(x):
    return jax.nn.sigmoid(x)

def _layernorm(x, axis=-1, eps=1e-05):
    m = jnp.mean(x, axis=axis, keepdims=True)
    v = jnp.var(x, axis=axis, keepdims=True)
    return (x - m) / jnp.sqrt(v + eps)

def _scatter_add(tgt, idx, src, axis=0):
    return tgt.at[idx].add(src)

def _segment_sum(src, seg, n):
    return jax.ops.segment_sum(src, seg, n)
kernel_name = 'mk_dlrm_tower_d1_rec_r8_f6beb6'

def setup_inputs(seed: int=0):
    np.random.seed(seed)
    _w = jnp.asarray

    def _rec_inputs():
        import jax
        import jax.numpy as jnp
        _tk = jax.random.key(seed)
        dense_ctx = jax.random.normal(jax.random.fold_in(_tk, 190), (2048, 16), jnp.float32)
        ids = jnp.stack([jax.random.randint(jax.random.fold_in(_tk, 200 + f), (2048,), 0, v, jnp.int32) for f, v in enumerate([1250, 1250, 1000, 1000, 125000, 125000, 1250, 12500, 12500, 125000, 1000, 1000, 125000, 1250, 1000, 1250, 12500, 1000, 1250, 1000, 12500, 1000, 12500, 1250, 1000, 12500, 12500, 1000, 125000, 12500, 1000, 1000, 12500, 12500, 1000, 1000, 1250, 125000, 12500, 12500])], axis=1)
        tbl_0 = 0.05 * jax.random.normal(jax.random.fold_in(_tk, 500 + 0), (1250, 32), jnp.float32)
        tbl_1 = 0.05 * jax.random.normal(jax.random.fold_in(_tk, 500 + 1), (1250, 32), jnp.float32)
        tbl_2 = 0.05 * jax.random.normal(jax.random.fold_in(_tk, 500 + 2), (1000, 32), jnp.float32)
        tbl_3 = 0.05 * jax.random.normal(jax.random.fold_in(_tk, 500 + 3), (1000, 32), jnp.float32)
        tbl_4 = 0.05 * jax.random.normal(jax.random.fold_in(_tk, 500 + 4), (125000, 32), jnp.float32)
        tbl_5 = 0.05 * jax.random.normal(jax.random.fold_in(_tk, 500 + 5), (125000, 32), jnp.float32)
        tbl_6 = 0.05 * jax.random.normal(jax.random.fold_in(_tk, 500 + 6), (1250, 32), jnp.float32)
        tbl_7 = 0.05 * jax.random.normal(jax.random.fold_in(_tk, 500 + 7), (12500, 32), jnp.float32)
        tbl_8 = 0.05 * jax.random.normal(jax.random.fold_in(_tk, 500 + 8), (12500, 32), jnp.float32)
        tbl_9 = 0.05 * jax.random.normal(jax.random.fold_in(_tk, 500 + 9), (125000, 32), jnp.float32)
        tbl_10 = 0.05 * jax.random.normal(jax.random.fold_in(_tk, 500 + 10), (1000, 32), jnp.float32)
        tbl_11 = 0.05 * jax.random.normal(jax.random.fold_in(_tk, 500 + 11), (1000, 32), jnp.float32)
        tbl_12 = 0.05 * jax.random.normal(jax.random.fold_in(_tk, 500 + 12), (125000, 32), jnp.float32)
        tbl_13 = 0.05 * jax.random.normal(jax.random.fold_in(_tk, 500 + 13), (1250, 32), jnp.float32)
        tbl_14 = 0.05 * jax.random.normal(jax.random.fold_in(_tk, 500 + 14), (1000, 32), jnp.float32)
        tbl_15 = 0.05 * jax.random.normal(jax.random.fold_in(_tk, 500 + 15), (1250, 32), jnp.float32)
        tbl_16 = 0.05 * jax.random.normal(jax.random.fold_in(_tk, 500 + 16), (12500, 32), jnp.float32)
        tbl_17 = 0.05 * jax.random.normal(jax.random.fold_in(_tk, 500 + 17), (1000, 32), jnp.float32)
        tbl_18 = 0.05 * jax.random.normal(jax.random.fold_in(_tk, 500 + 18), (1250, 32), jnp.float32)
        tbl_19 = 0.05 * jax.random.normal(jax.random.fold_in(_tk, 500 + 19), (1000, 32), jnp.float32)
        tbl_20 = 0.05 * jax.random.normal(jax.random.fold_in(_tk, 500 + 20), (12500, 32), jnp.float32)
        tbl_21 = 0.05 * jax.random.normal(jax.random.fold_in(_tk, 500 + 21), (1000, 32), jnp.float32)
        tbl_22 = 0.05 * jax.random.normal(jax.random.fold_in(_tk, 500 + 22), (12500, 32), jnp.float32)
        tbl_23 = 0.05 * jax.random.normal(jax.random.fold_in(_tk, 500 + 23), (1250, 32), jnp.float32)
        tbl_24 = 0.05 * jax.random.normal(jax.random.fold_in(_tk, 500 + 24), (1000, 32), jnp.float32)
        tbl_25 = 0.05 * jax.random.normal(jax.random.fold_in(_tk, 500 + 25), (12500, 32), jnp.float32)
        tbl_26 = 0.05 * jax.random.normal(jax.random.fold_in(_tk, 500 + 26), (12500, 32), jnp.float32)
        tbl_27 = 0.05 * jax.random.normal(jax.random.fold_in(_tk, 500 + 27), (1000, 32), jnp.float32)
        tbl_28 = 0.05 * jax.random.normal(jax.random.fold_in(_tk, 500 + 28), (125000, 32), jnp.float32)
        tbl_29 = 0.05 * jax.random.normal(jax.random.fold_in(_tk, 500 + 29), (12500, 32), jnp.float32)
        tbl_30 = 0.05 * jax.random.normal(jax.random.fold_in(_tk, 500 + 30), (1000, 32), jnp.float32)
        tbl_31 = 0.05 * jax.random.normal(jax.random.fold_in(_tk, 500 + 31), (1000, 32), jnp.float32)
        tbl_32 = 0.05 * jax.random.normal(jax.random.fold_in(_tk, 500 + 32), (12500, 32), jnp.float32)
        tbl_33 = 0.05 * jax.random.normal(jax.random.fold_in(_tk, 500 + 33), (12500, 32), jnp.float32)
        tbl_34 = 0.05 * jax.random.normal(jax.random.fold_in(_tk, 500 + 34), (1000, 32), jnp.float32)
        tbl_35 = 0.05 * jax.random.normal(jax.random.fold_in(_tk, 500 + 35), (1000, 32), jnp.float32)
        tbl_36 = 0.05 * jax.random.normal(jax.random.fold_in(_tk, 500 + 36), (1250, 32), jnp.float32)
        tbl_37 = 0.05 * jax.random.normal(jax.random.fold_in(_tk, 500 + 37), (125000, 32), jnp.float32)
        tbl_38 = 0.05 * jax.random.normal(jax.random.fold_in(_tk, 500 + 38), (12500, 32), jnp.float32)
        tbl_39 = 0.05 * jax.random.normal(jax.random.fold_in(_tk, 500 + 39), (12500, 32), jnp.float32)
        _rk = jax.random.fold_in(_tk, 7)
        W_top1 = 0.176777 * jax.random.normal(jax.random.fold_in(_tk, 801), (32, 512), jnp.float32)
        W_top2 = 0.0441942 * jax.random.normal(jax.random.fold_in(_tk, 802), (512, 256), jnp.float32)
        W_top3 = 0.0625 * jax.random.normal(jax.random.fold_in(_tk, 803), (256, 1), jnp.float32)
        b_top1 = jnp.zeros((512,), jnp.float32)
        b_top2 = jnp.zeros((256,), jnp.float32)
        return (dense_ctx, ids, tbl_0, tbl_1, tbl_2, tbl_3, tbl_4, tbl_5, tbl_6, tbl_7, tbl_8, tbl_9, tbl_10, tbl_11, tbl_12, tbl_13, tbl_14, tbl_15, tbl_16, tbl_17, tbl_18, tbl_19, tbl_20, tbl_21, tbl_22, tbl_23, tbl_24, tbl_25, tbl_26, tbl_27, tbl_28, tbl_29, tbl_30, tbl_31, tbl_32, tbl_33, tbl_34, tbl_35, tbl_36, tbl_37, tbl_38, tbl_39, W_top1, b_top1, W_top2, b_top2, W_top3)
    dense_ctx, ids, tbl_0, tbl_1, tbl_2, tbl_3, tbl_4, tbl_5, tbl_6, tbl_7, tbl_8, tbl_9, tbl_10, tbl_11, tbl_12, tbl_13, tbl_14, tbl_15, tbl_16, tbl_17, tbl_18, tbl_19, tbl_20, tbl_21, tbl_22, tbl_23, tbl_24, tbl_25, tbl_26, tbl_27, tbl_28, tbl_29, tbl_30, tbl_31, tbl_32, tbl_33, tbl_34, tbl_35, tbl_36, tbl_37, tbl_38, tbl_39, W_top1, b_top1, W_top2, b_top2, W_top3 = _rec_inputs()

    def _L0_rec_setup():
        import jax, jax.numpy as jnp
        import numpy as np
        import itertools
        LN_EPS = 0.001

        def _pair_indices(field_num):
            pairs = np.array(list(itertools.combinations(range(field_num), 2)), dtype=np.int32)
            return (pairs[:, 0], pairs[:, 1])
        key = jax.random.key(seed)
        ks = jax.random.split(key, 3)
        B, F, E, P, D = (256, 40, 32, 780, 16)
        x = jax.random.normal(ks[0], (B, F, E), dtype=jnp.float32)
        W = jax.random.normal(ks[1], (P, E, E), dtype=jnp.float32) * (2.0 / (E + E)) ** 0.5
        dense_w = jax.random.normal(ks[2], (P, D), dtype=jnp.float32) * (2.0 / (P + D)) ** 0.5
        dense_b = jnp.zeros((D,), dtype=jnp.float32)
        gamma = jnp.ones((D,), dtype=jnp.float32)
        beta = jnp.zeros((D,), dtype=jnp.float32)
        return {'x': x, 'W': W, 'dense_w': dense_w, 'dense_b': dense_b, 'gamma': gamma, 'beta': beta}
    _L0_rec_all = _L0_rec_setup()
    _L0_rec_in = {k: v for k, v in _L0_rec_all.items() if k in ('W', 'dense_w', 'dense_b', 'gamma', 'beta')}
    del _L0_rec_all
    return {'dense_ctx': dense_ctx, 'ids': ids, 'tbl_0': tbl_0, 'tbl_1': tbl_1, 'tbl_2': tbl_2, 'tbl_3': tbl_3, 'tbl_4': tbl_4, 'tbl_5': tbl_5, 'tbl_6': tbl_6, 'tbl_7': tbl_7, 'tbl_8': tbl_8, 'tbl_9': tbl_9, 'tbl_10': tbl_10, 'tbl_11': tbl_11, 'tbl_12': tbl_12, 'tbl_13': tbl_13, 'tbl_14': tbl_14, 'tbl_15': tbl_15, 'tbl_16': tbl_16, 'tbl_17': tbl_17, 'tbl_18': tbl_18, 'tbl_19': tbl_19, 'tbl_20': tbl_20, 'tbl_21': tbl_21, 'tbl_22': tbl_22, 'tbl_23': tbl_23, 'tbl_24': tbl_24, 'tbl_25': tbl_25, 'tbl_26': tbl_26, 'tbl_27': tbl_27, 'tbl_28': tbl_28, 'tbl_29': tbl_29, 'tbl_30': tbl_30, 'tbl_31': tbl_31, 'tbl_32': tbl_32, 'tbl_33': tbl_33, 'tbl_34': tbl_34, 'tbl_35': tbl_35, 'tbl_36': tbl_36, 'tbl_37': tbl_37, 'tbl_38': tbl_38, 'tbl_39': tbl_39, 'W_top1': W_top1, 'b_top1': b_top1, 'W_top2': W_top2, 'b_top2': b_top2, 'W_top3': W_top3, 'L0_rec_W': _L0_rec_in['W'], 'L0_rec_dense_w': _L0_rec_in['dense_w'], 'L0_rec_dense_b': _L0_rec_in['dense_b'], 'L0_rec_gamma': _L0_rec_in['gamma'], 'L0_rec_beta': _L0_rec_in['beta']}

def reference(dense_ctx, ids, tbl_0, tbl_1, tbl_2, tbl_3, tbl_4, tbl_5, tbl_6, tbl_7, tbl_8, tbl_9, tbl_10, tbl_11, tbl_12, tbl_13, tbl_14, tbl_15, tbl_16, tbl_17, tbl_18, tbl_19, tbl_20, tbl_21, tbl_22, tbl_23, tbl_24, tbl_25, tbl_26, tbl_27, tbl_28, tbl_29, tbl_30, tbl_31, tbl_32, tbl_33, tbl_34, tbl_35, tbl_36, tbl_37, tbl_38, tbl_39, W_top1, b_top1, W_top2, b_top2, W_top3, L0_rec_W, L0_rec_dense_w, L0_rec_dense_b, L0_rec_gamma, L0_rec_beta):
    import jax
    import jax.numpy as jnp

    def _L0_rec_ref(x, W, dense_w, dense_b, gamma, beta):
        import jax, jax.numpy as jnp
        import numpy as np
        import itertools
        LN_EPS = 0.001

        def _pair_indices(field_num):
            pairs = np.array(list(itertools.combinations(range(field_num), 2)), dtype=np.int32)
            return (pairs[:, 0], pairs[:, 1])
        F = x.shape[1]
        idx_i, idx_j = _pair_indices(F)
        xi = x[:, idx_i, :]
        xj = x[:, idx_j, :]
        t = jnp.einsum('bpe,pef->bpf', xi, W)
        p = jnp.einsum('bpf,bpf->bp', t, xj)
        h = p @ dense_w + dense_b
        mu = jnp.mean(h, axis=-1, keepdims=True)
        var = jnp.mean(jnp.square(h - mu), axis=-1, keepdims=True)
        out = (h - mu) * jax.lax.rsqrt(var + LN_EPS) * gamma + beta
        return out
    e = jnp.stack([tbl_0[ids[:, 0]], tbl_1[ids[:, 1]], tbl_2[ids[:, 2]], tbl_3[ids[:, 3]], tbl_4[ids[:, 4]], tbl_5[ids[:, 5]], tbl_6[ids[:, 6]], tbl_7[ids[:, 7]], tbl_8[ids[:, 8]], tbl_9[ids[:, 9]], tbl_10[ids[:, 10]], tbl_11[ids[:, 11]], tbl_12[ids[:, 12]], tbl_13[ids[:, 13]], tbl_14[ids[:, 14]], tbl_15[ids[:, 15]], tbl_16[ids[:, 16]], tbl_17[ids[:, 17]], tbl_18[ids[:, 18]], tbl_19[ids[:, 19]], tbl_20[ids[:, 20]], tbl_21[ids[:, 21]], tbl_22[ids[:, 22]], tbl_23[ids[:, 23]], tbl_24[ids[:, 24]], tbl_25[ids[:, 25]], tbl_26[ids[:, 26]], tbl_27[ids[:, 27]], tbl_28[ids[:, 28]], tbl_29[ids[:, 29]], tbl_30[ids[:, 30]], tbl_31[ids[:, 31]], tbl_32[ids[:, 32]], tbl_33[ids[:, 33]], tbl_34[ids[:, 34]], tbl_35[ids[:, 35]], tbl_36[ids[:, 36]], tbl_37[ids[:, 37]], tbl_38[ids[:, 38]], tbl_39[ids[:, 39]]], axis=1)
    z = _L0_rec_ref(e, L0_rec_W, L0_rec_dense_w, L0_rec_dense_b, L0_rec_gamma, L0_rec_beta)
    z = z.reshape(z.shape[0], -1)
    h = jnp.concatenate([z, dense_ctx], axis=1)
    h = jnp.maximum(h @ W_top1 + b_top1, 0.0)
    h = jnp.maximum(h @ W_top2 + b_top2, 0.0)
    y = h @ W_top3
    return y

_drawn_inputs = setup_inputs


def setup_inputs(seed=0):
    import zlib

    import numpy as np

    out = dict(_drawn_inputs(seed))
    spreads = {'b_top1': (0.0, 0.1),
     'b_top2': (0.0, 0.1),
     'L0_rec_dense_b': (0.0, 0.1),
     'L0_rec_gamma': (1.0, 0.2),
     'L0_rec_beta': (0.0, 0.1)}
    factors = {}
    for name, (base, spread) in spreads.items():
        noise = np.random.default_rng([zlib.crc32(name.encode()), seed]).standard_normal(out[name].shape)
        drawn = base * np.exp(spread * noise) if base else spread * noise
        out[name] = jnp.asarray(drawn.astype(out[name].dtype))
    for name, factor in factors.items():
        out[name] = (out[name] * factor).astype(out[name].dtype)
    return out
```

```python
import concourse.bass as bass
from concourse import mybir
from contextlib import ExitStack

F32 = mybir.dt.float32
F32R = mybir.dt.float32r
I32 = mybir.dt.int32
ALU = mybir.AluOpType
ACT = mybir.ActivationFunctionType

P = 128
FIELDS = 40
E = 32
GROUP = 4
OCTET = 8
GROUPS = FIELDS // GROUP
OCTETS = FIELDS // OCTET
D = 16
LN_EPS = 1e-3
BS = 256
BT = BS // P


def field_units(j):
    octet, r = divmod(j, OCTET)
    doubles = octet + (1 if r > GROUP else 0)
    single = 1 <= r <= GROUP
    return doubles, single


def plan():
    tiles, unit_at, double_at, single_at = [], [], [], []
    units = doubles = singles = 0
    for j in range(FIELDS):
        nd, single = field_units(j)
        unit_at.append(units)
        double_at.append(doubles)
        single_at.append(singles)
        mine = [[d, min(2, nd - d), False] for d in range(0, nd, 2)]
        if single and mine and mine[-1][1] == 1:
            mine[-1][2] = True
        elif single:
            mine.append([nd, 0, True])
        tiles += [(j, *t) for t in mine]
        units += 2 * nd + single
        doubles += nd
        singles += single
    return tiles, unit_at, double_at, single_at, units, doubles, singles


TILES, UNIT_AT, DOUBLE_AT, SINGLE_AT, UNITS, DOUBLES, SINGLES = plan()
NT = len(TILES)
TILE_UNITS = 4
SUM_RING = 3
assert NT % 2 == 1 and NT % SUM_RING == 0
TILES_BEFORE = [sum(t[0] < j for t in TILES) for j in range(FIELDS + 1)]
SUMS_BEFORE = [sum(t[2] > 0 for t in TILES[:i]) for i in range(NT + 1)]
NSUM = SUMS_BEFORE[NT]

PIECES = 14
PIECE = UNITS // PIECES * P
assert UNITS % PIECES == 0

FRONT_AT = [38] + [GROUP * g - 2 for g in range(1, GROUPS)]
SPLIT_AT = {3: 8, 4: 12, 5: 16, 6: 20, 7: 24, 8: 28, 9: 31}
SPLIT_NEXT_AT = {0: 34, 1: 36, 2: 37}
MLP_AT = {10: "center", 12: "variance", 15: "up_low", 17: "up_high", 19: "middle", 21: "out"}
MLP_NORM_AT = 13
MLP_STAGES = 6
XS_RING = 5


def interaction_tower(nc, ids, tables, w_units, dw_doubles, dw_singles, dense_b, gamma, beta, ctx_t,
                      w1, b1, w2, b2, w3, out):
    B = ids.shape[0]
    BLOCKS = B // BS
    H1, H2 = w2.shape
    M1, M2 = H1 // P, H2 // P
    C = w1.shape[0]
    assert BLOCKS >= 4 and BLOCKS % 2 == 0 and M1 == 4 and M2 == 2

    with ExitStack() as ctx:
        def sb(name, shape, dt=F32):
            return ctx.enter_context(nc.sbuf_tensor(name, shape, dt))

        def sem(name):
            return ctx.enter_context(nc.semaphore(name))

        w_split = sb("w_split", [P, UNITS * P], F32R)
        dwd = sb("dwd", [P, DOUBLES, D])
        dws = sb("dws", [P, SINGLES, D])
        windows = sb("windows", [P, 2, 2 * OCTETS + OCTETS, BS])
        movers = sb("movers", [P, 2, GROUP, BS], F32R)
        x_nat = sb("x_nat", [P, OCTETS, BT, OCTET * E])
        x_split = sb("x_split", [P, XS_RING, BT, GROUP, 2, E], F32R)
        products = sb("products", [P, 2, TILE_UNITS, BS])
        sums = sb("sums", [P, SUM_RING, 3, BS])
        ids_sb = sb("ids_sb", [P, 2, BT, FIELDS], I32)
        identity = sb("identity", [P, P])
        identity_r = sb("identity_r", [P, P], F32R)
        centering = sb("centering", [D, D])
        averaging = sb("averaging", [D, D])
        db_sb, gamma_sb, beta_sb = sb("db_sb", [D, 1]), sb("gamma_sb", [D, 1]), sb("beta_sb", [D, 1])
        w1_sb = sb("w1_sb", [C, H1])
        w2_sb = sb("w2_sb", [P, M1, H2])
        w3_sb = sb("w3_sb", [P, M2])
        b1_sb, b2_sb = sb("b1_sb", [P, M1]), sb("b2_sb", [P, M2])
        h_sb, hc_sb, sq_sb = sb("h_sb", [D, BS]), sb("hc_sb", [D, BS]), sb("sq_sb", [D, BS])
        std_sb, rstd_sb = h_sb, sq_sb
        eps_sb = sb("eps_sb", [D, 1])
        z_cat = sb("z_cat", [C, 2, BS])
        a1 = sb("a1", [P, M1, BS])
        a2 = sb("a2", [P, M2, BS])
        y_sb = sb("y_sb", [1, BS])
        stage_flat = windows[:, 1, :, :].rearrange("p u b -> p (u b)")
        staging = [stage_flat[:, s * PIECE:(s + 1) * PIECE] for s in range(2)]
        assert 2 * PIECE <= 3 * OCTETS * BS

        t_ps = ctx.enter_context(nc.psum_tensor("t_ps", [P, 2, TILE_UNITS, BS], F32))
        mover_ps = ctx.enter_context(nc.psum_tensor("mover_ps", [P, 2, BS], F32))
        window_ps = ctx.enter_context(nc.psum_tensor("window_ps", [P, 2, BS], F32))
        h_ps = ctx.enter_context(nc.psum_tensor("h_ps", [P, 2 * BS], F32))
        mlp_ps = ctx.enter_context(nc.psum_tensor("mlp_ps", [P, 2, BS], F32))

        weights_in = [sem(f"weights_in{s}") for s in range(2)]
        dense_in = sem("dense_in")
        params_in = sem("params_in")
        ids_in = [sem(f"ids_in{s}") for s in range(2)]
        context_in = [sem(f"context_in{s}") for s in range(2)]
        gathered = [sem(f"gathered{g}") for g in range(GROUPS)]
        high_weights = sem("high_weights")
        low_weights = sem("low_weights")
        constants = sem("constants")
        identity_rounded = sem("identity_rounded")
        high_split = sem("high_split")
        low_split = sem("low_split")
        movers_transposed = sem("movers_transposed")
        windows_transposed = sem("windows_transposed")
        movers_ready = sem("movers_ready")
        windows_ready = sem("windows_ready")
        t_ready = sem("t_ready")
        multiplied = sem("multiplied")
        added = sem("added")
        contracted = sem("contracted")
        h_copied = sem("h_copied")
        mlp_mm = sem("mlp_mm")
        mlp_act = sem("mlp_act")
        normed = sem("normed")
        out_done = sem("out_done")

        def rows_of(g):
            return x_nat[:, g // 2, :, g % 2 * GROUP * E:(g % 2 + 1) * GROUP * E]

        block = ctx.enter_context(nc.Block())

        class Step:

            def __init__(self, k, half, parity, first=False, last=False):
                self.k, self.half, self.parity, self.first, self.last = k, half, parity, first, last

            def before(self):
                return Step(self.k - 1, self.half - (1 - self.parity), 1 - self.parity)

            def after(self):
                return Step(self.k + 1, self.half + self.parity, 1 - self.parity)

        def each_block(engine, emit):
            emit(Step(0, 0, 0, first=True))
            with engine.Fori(0, BLOCKS // 2 - 1) as i:
                emit(Step(2 * i + 1, i, 1))
                emit(Step(2 * i + 2, i + 1, 0))
            emit(Step(BLOCKS - 1, BLOCKS // 2 - 1, 1, last=True))

        ACT_STEPS = 9
        NORM_STEPS = 3

        @block.sync
        def _(sp):
            for piece in range(PIECES):
                s = piece % 2
                if piece >= 2:
                    sp.wait_ge(high_weights, piece - 1)
                    sp.wait_ge(low_weights, piece - 1)
                for copy in range(4):
                    sp.dma_start(staging[s][copy * E:(copy + 1) * E, :],
                                 w_units[:, piece * PIECE:(piece + 1) * PIECE]).then_inc(weights_in[s], 16)

        @block.gpsimd
        def _(pool):
            pool.memset(identity[:], 0.0).then_inc(constants, 1)
            pool.memset(centering[:], -1.0 / D).then_inc(constants, 1)
            pool.memset(averaging[:], 1.0 / D).then_inc(constants, 1)
            pool.memset(eps_sb[:], LN_EPS).then_inc(constants, 1)
            pool.wait_ge(constants, 4)
            pool.affine_select(out=identity[:], in_=identity[:], compare_op=ALU.not_equal, fill=1.0, base=0,
                               pattern=[[-1, P]], channel_multiplier=1).then_inc(constants, 1)
            pool.affine_select(out=centering[:], in_=centering[:], compare_op=ALU.not_equal,
                               fill=1.0 - 1.0 / D, base=0, pattern=[[-1, D]], channel_multiplier=1
                               ).then_inc(constants, 1)

            def wait_for_slot(b, g):
                if g == 0:
                    pool.wait_ge(ids_in[b.parity], 16 * (b.half + 1))
                if not b.first:
                    pool.wait_ge(high_split, GROUPS * (b.k - 1) + g + 1)
                    pool.wait_ge(low_split, GROUPS * (b.k - 1) + g + 1)
                    pool.wait_ge(windows_transposed, GROUPS * (b.k - 1) + (g | 1) + 1)

            def gather(b, g):
                for t in range(BT):
                    for f in range(GROUP):
                        field = GROUP * g + f
                        pool.indirect_dma_start(
                            rows_of(g)[:, t, f * E:(f + 1) * E], None, tables[field][:, :],
                            bass.IndirectOffsetOnAxis(ap=ids_sb[:, b.parity, t, field:field + 1], axis=0)
                        ).then_inc(gathered[g], 16)

            def split_low(b, g):
                seq = GROUPS * b.k + g
                pool.wait_ge(gathered[g], BT * GROUP * 16 * (b.k + 1))
                pool.wait_ge(high_split, seq + 1)
                xs = x_split[:, g % XS_RING, :, :, :, :]
                pool.tensor_tensor(xs[:, :, :, 1, :],
                                   rows_of(g).rearrange("p t (f e) -> p t f e", e=E),
                                   xs[:, :, :, 0, :].bitcast(F32),
                                   ALU.subtract).then_inc(low_split, 1)

            LAG = 2

            def emit(b):
                for g in range(GROUPS):
                    wait_for_slot(b, g)
                    if g >= LAG:
                        split_low(b, g - LAG)
                    elif not b.first:
                        split_low(b.before(), g - LAG + GROUPS)
                    gather(b, g)

            each_block(pool, emit)
            final = Step(BLOCKS - 1, BLOCKS // 2 - 1, 1)
            for g in range(GROUPS - LAG, GROUPS):
                split_low(final, g)

        @block.scalar
        def _(act):
            def load_ids(b):
                act.dma_start(ids_sb[:, b.parity, :, :],
                              ids[bass.ds(b.k * BS, BS), :].rearrange("(t p) f -> p t f", p=P)
                              ).then_inc(ids_in[b.parity], 16)

            def load_context(b):
                act.dma_start(z_cat[D:C, b.parity, :], ctx_t[:, bass.ds(b.k * BS, BS)]
                              ).then_inc(context_in[b.parity], 16)

            load_ids(Step(0, 0, 0))
            for dst, src in ((db_sb, dense_b), (gamma_sb, gamma), (beta_sb, beta)):
                act.dma_start(dst[:, :], src.rearrange("(d o) -> d o", o=1)).then_inc(params_in, 16)
            for s in range(OCTET):
                act.dma_start(dwd[s * D:(s + 1) * D, :, :],
                              dw_doubles[s:s + 1, :, :].broadcast_to([D, DOUBLES, D])).then_inc(dense_in, 16)
            for s in range(GROUP):
                act.dma_start(dws[s * E:(s + 1) * E, :, :],
                              dw_singles[s:s + 1, :, :].broadcast_to([E, SINGLES, D])).then_inc(dense_in, 16)
            act.dma_start(w1_sb[:, :], w1).then_inc(params_in, 16)
            act.dma_start(w2_sb[:, :, :], w2.rearrange("(m p) n -> p m n", p=P)).then_inc(params_in, 16)
            act.dma_start(w3_sb[:, :], w3).then_inc(params_in, 16)
            act.dma_start(b1_sb[:, :], b1).then_inc(params_in, 16)
            act.dma_start(b2_sb[:, :], b2).then_inc(params_in, 16)

            def split_high(b, g):
                act.wait_ge(gathered[g], BT * GROUP * 16 * (b.k + 1))
                if not b.first or g >= XS_RING:
                    act.wait_ge(movers_transposed, GROUPS * b.k + g - XS_RING + 1)
                xs = x_split[:, g % XS_RING, :, :, :, :]
                act.activation(xs[:, :, :, 0, :],
                               rows_of(g).rearrange("p t (f e) -> p t f e", e=E),
                               ACT.Copy).then_inc(high_split, 1)

            def evacuate(b, g):
                seq = GROUPS * b.k + g
                act.wait_ge(movers_transposed, seq + 1)
                if not b.first or g >= 2:
                    behind = b if g >= 2 else b.before()
                    act.wait_ge(t_ready, NT * behind.k + TILES_BEFORE[GROUP * ((g - 2) % GROUPS + 1)])
                slot = movers[:, g % 2, :, :].rearrange("p (a c) b -> p a c b", c=2)
                for odd in range(2):
                    for half in range(2):
                        last = act.activation(slot[half * 64:(half + 1) * 64, :, odd, :],
                                              mover_ps[odd * 64:(odd + 1) * 64, :, :], ACT.Copy)
                last.then_inc(movers_ready, 1)
                act.wait_ge(windows_transposed, seq + 1)
                octet = g // 2
                if g == 0 and not b.first:
                    act.wait_ge(multiplied, NT * (b.k - 1) + 1)
                if g % 2 == 0:
                    act.activation(windows[:, b.parity, 2 * OCTETS + octet, :], window_ps[:, 0, :], ACT.Copy
                                   ).then_inc(windows_ready, 1)
                else:
                    act.activation(windows[:, b.parity, 2 * octet:2 * octet + 2, :], window_ps[:, :, :],
                                   ACT.Copy).then_inc(windows_ready, 1)

            def mlp(b, stage):
                stage_no = list(MLP_AT.values()).index(stage)
                act.wait_ge(mlp_mm, MLP_STAGES * b.k + stage_no + 1)
                done = ACT_STEPS * b.k
                if stage == "center":
                    act.activation(sq_sb[:, :], mlp_ps[0:D, 0, :], ACT.Square).then_inc(mlp_act, 1)
                    act.activation(hc_sb[:, :], mlp_ps[0:D, 0, :], ACT.Copy).then_inc(mlp_act, 1)
                elif stage == "variance":
                    act.activation(std_sb[:, :], mlp_ps[0:D, 0, :], ACT.Sqrt, bias=eps_sb[:, :]
                                   ).then_inc(mlp_act, 1)
                elif stage in ("up_low", "up_high"):
                    for m in range(2):
                        c = 2 * (stage == "up_high") + m
                        act.activation(a1[:, c, :], mlp_ps[:, m, :], ACT.Relu, bias=b1_sb[:, c:c + 1]
                                       ).then_inc(mlp_act, 1)
                elif stage == "middle":
                    for m in range(2):
                        last = act.activation(a2[:, m, :], mlp_ps[:, m, :], ACT.Relu,
                                              bias=b2_sb[:, m:m + 1])
                    last.then_inc(mlp_act, 1)
                else:
                    act.activation(y_sb[:, :], mlp_ps[0:1, 0, :], ACT.Copy).then_inc(mlp_act, 1)
                    act.wait_ge(mlp_act, done + ACT_STEPS)
                    act.dma_start(out[bass.ds(b.k * BS, BS), :].rearrange("b o -> o b"), y_sb[:, :]
                                  ).then_inc(out_done, 16)

            def copy_h(b):
                act.wait_ge(contracted, NT * (b.k + 1))
                act.activation(h_sb[:, :], h_ps[32 * b.parity:32 * b.parity + D, 0:BS], ACT.Identity,
                               bias=db_sb[:, :]).then_inc(h_copied, 1)

            act.wait_ge(constants, 6)
            act.activation(identity_r[:, :], identity[:, :], ACT.Copy).then_inc(identity_rounded, 1)
            split_at_piece = {3: 0, 6: 1, 9: 2}
            for piece in range(PIECES):
                s = piece % 2
                act.wait_ge(weights_in[s], 64 * (piece // 2 + 1))
                act.activation(w_split[:, piece * PIECE:(piece + 1) * PIECE], staging[s][:, :], ACT.Copy
                               ).then_inc(high_weights, 1)
                if piece in split_at_piece:
                    split_high(Step(0, 0, 0, first=True), split_at_piece[piece])
            evacuate(Step(0, 0, 0, first=True), 0)
            act.wait_ge(params_in, 8 * 16)

            def emit(b):
                if not b.last:
                    load_ids(b.after())
                load_context(b)
                for j in range(FIELDS):
                    if j == 6 and not b.first:
                        copy_h(b.before())
                    if j == 33 and not b.first:
                        act.wait_ge(out_done, 16 * b.k)
                    if j in MLP_AT and not b.first:
                        mlp(b.before(), MLP_AT[j])
                    for g in range(GROUPS):
                        if SPLIT_AT.get(g) == j:
                            split_high(b, g)
                        if SPLIT_NEXT_AT.get(g) == j and not b.last:
                            split_high(b.after(), g)
                        if FRONT_AT[g] == j and g > 0:
                            evacuate(b, g)
                    if j == FRONT_AT[0] and not b.last:
                        evacuate(b.after(), 0)

            each_block(act, emit)
            final = Step(BLOCKS - 1, BLOCKS // 2 - 1, 1)
            copy_h(final)
            for stage in MLP_AT.values():
                mlp(final, stage)
            act.wait_ge(out_done, 16 * BLOCKS)

        @block.vector
        def _(dve):
            for piece in range(PIECES):
                s = piece % 2
                dve.wait_ge(weights_in[s], 64 * (piece // 2 + 1))
                dve.wait_ge(high_weights, piece + 1)
                part = w_split[64:P, piece * PIECE:(piece + 1) * PIECE]
                dve.tensor_tensor(part, staging[s][64:P, :], part.bitcast(F32), ALU.subtract
                                  ).then_inc(low_weights, 1)
            dve.wait_ge(params_in, 8 * 16)

            def multiply(b, i):
                j, d0, nd, single = TILES[i]
                octet = j // OCTET
                n = NT * b.k + i
                dve.wait_ge(t_ready, n + 1)
                if TILES_BEFORE[j] == i:
                    dve.wait_ge(windows_ready, GROUPS * b.k + j // GROUP + 1)
                slot = (i + b.parity) % 2
                work = []
                if nd:
                    if not b.first or i >= 2:
                        behind = SUMS_BEFORE[i - 1] if i >= 2 else SUMS_BEFORE[NT - 1 + i] - NSUM
                        dve.wait_ge(added, NSUM * b.k + behind)
                    work.append((products[:, slot, 0:2 * nd, :], t_ps[:, slot, 0:2 * nd, :],
                                 windows[:, b.parity, 2 * d0:2 * (d0 + nd), :]))
                if single:
                    if not b.first or i >= SUM_RING:
                        dve.wait_ge(contracted, n + 1 - SUM_RING)
                    work.append((sums[:, i % SUM_RING, 2, :], t_ps[:, slot, 2 * nd, :],
                                 windows[:, b.parity, 2 * OCTETS + octet, :]))
                for dst, a, w in work:
                    last = dve.tensor_tensor(dst, a, w, ALU.mult)
                last.then_inc(multiplied, 1)

            def add(b, i):
                _, _, nd, _ = TILES[i]
                if not nd:
                    return
                n = NT * b.k + i
                dve.wait_ge(multiplied, n + 1)
                if not isinstance(n, int) or n >= SUM_RING:
                    dve.wait_ge(contracted, n + 1 - SUM_RING)
                pair = products[:, (i + b.parity) % 2, 0:2 * nd, :].rearrange("p (d h) b -> p d h b", h=2)
                dve.tensor_tensor(sums[:, i % SUM_RING, 0:nd, :], pair[:, :, 0, :], pair[:, :, 1, :], ALU.add
                                  ).then_inc(added, 1)

            def norm(b):
                dve.wait_ge(mlp_act, ACT_STEPS * b.k + 3)
                dve.reciprocal(rstd_sb[:, :], std_sb[:, :]).then_inc(normed, 1)
                dve.wait_ge(normed, NORM_STEPS * b.k + 1)
                dve.tensor_tensor(rstd_sb[:, :], hc_sb[:, :], rstd_sb[:, :], ALU.mult).then_inc(normed, 1)
                dve.wait_ge(normed, NORM_STEPS * b.k + 2)
                dve.tensor_scalar(z_cat[0:D, b.parity, :], rstd_sb[:, :], gamma_sb[:, :], beta_sb[:, :],
                                  ALU.mult, ALU.add).then_inc(normed, 1)

            def emit(b):
                for i in range(NT):
                    if i == TILES_BEFORE[MLP_NORM_AT] and not b.first:
                        norm(b.before())
                    multiply(b, i)
                    if i >= 1:
                        add(b, i - 1)
                    elif not b.first:
                        add(b.before(), NT - 1)

            each_block(dve, emit)
            final = Step(BLOCKS - 1, BLOCKS // 2 - 1, 1)
            add(final, NT - 1)
            norm(final)

        @block.tensor
        def _(pe):
            CONTRACT_LAG = 3

            def transpose_group(b, g):
                seq = GROUPS * b.k + g
                pe.wait_ge(low_split, seq + 1)
                if not b.first or g >= 1:
                    pe.wait_ge(movers_ready, seq)
                for pair in range(2):
                    for t in range(BT):
                        last = pe.matmul(
                            mover_ps[:, pair, t * P:(t + 1) * P],
                            x_split[:, g % XS_RING, t, 2 * pair:2 * pair + 2, :, :].rearrange("p f h e -> p (f h e)"),
                            identity_r[:, :], start=True, stop=True)
                last.then_inc(movers_transposed, 1)
                if not b.first or g >= 1:
                    pe.wait_ge(windows_ready, seq)
                if g % 2 == 0:
                    pe.wait_ge(gathered[g], BT * GROUP * 16 * (b.k + 1))
                    for t in range(BT):
                        last = pe.transpose(window_ps[:, 0, t * P:(t + 1) * P], rows_of(g)[:, t, :], identity[:, :])
                else:
                    pe.wait_ge(gathered[g], BT * GROUP * 16 * (b.k + 1))
                    for half in range(2):
                        for t in range(BT):
                            last = pe.transpose(window_ps[:, half, t * P:(t + 1) * P],
                                                x_nat[:, g // 2, t, half::2], identity[:, :])
                last.then_inc(windows_transposed, 1)

            def interact(b, i):
                j, d0, nd, single = TILES[i]
                n = NT * b.k + i
                if TILES_BEFORE[j] == i:
                    pe.wait_ge(movers_ready, GROUPS * b.k + j // GROUP + 1)
                if not isinstance(n, int) or n >= 2:
                    pe.wait_ge(multiplied, n - 1)
                slot = (i + b.parity) % 2
                unit = UNIT_AT[j] + 2 * d0
                for u in range(2 * nd + single):
                    last = pe.matmul(t_ps[:, slot, u, :], w_split[:, (unit + u) * P:(unit + u + 1) * P],
                                     movers[:, j // GROUP % 2, j % GROUP, :], start=True, stop=True)
                last.then_inc(t_ready, 1)

            def contract(b, i):
                j, d0, nd, single = TILES[i]
                n = NT * b.k + i
                if nd:
                    pe.wait_ge(added, NSUM * b.k + SUMS_BEFORE[i + 1])
                if single:
                    pe.wait_ge(multiplied, n + 1)
                acc = h_ps[32 * b.parity:32 * b.parity + D, 0:BS]
                parts = [(dwd[:, DOUBLE_AT[j] + d0 + q, :], q) for q in range(nd)]
                if single:
                    parts.append((dws[:, SINGLE_AT[j], :], 2))
                for q, (dw, at) in enumerate(parts):
                    last = pe.matmul(acc, dw, sums[:, i % SUM_RING, at, :], start=(i == 0 and q == 0),
                                     stop=(i == NT - 1 and q == len(parts) - 1))
                last.then_inc(contracted, 1)

            def mlp_waits(b, stage):
                done = ACT_STEPS * b.k
                if stage == "center":
                    pe.wait_ge(h_copied, b.k + 1)
                elif stage == "variance":
                    pe.wait_ge(mlp_act, done + 2)

            def mlp(b, stage):
                done = ACT_STEPS * b.k
                if stage == "center":
                    last = pe.matmul(mlp_ps[0:D, 0, :], centering[:, :], h_sb[:, :], start=True, stop=True)
                elif stage == "variance":
                    last = pe.matmul(mlp_ps[0:D, 0, :], averaging[:, :], sq_sb[:, :], start=True, stop=True)
                elif stage in ("up_low", "up_high"):
                    if stage == "up_low":
                        pe.wait_ge(mlp_act, done + 3)
                        pe.wait_ge(normed, NORM_STEPS * (b.k + 1))
                        pe.wait_ge(context_in[b.parity], 16 * (b.half + 1))
                    else:
                        pe.wait_ge(mlp_act, done + 5)
                    for m in range(2):
                        c = 2 * (stage == "up_high") + m
                        last = pe.matmul(mlp_ps[:, m, :], w1_sb[:, c * P:(c + 1) * P], z_cat[:, b.parity, :],
                                         start=True, stop=True)
                elif stage == "middle":
                    pe.wait_ge(mlp_act, done + 7)
                    for m in range(M2):
                        for c in range(M1):
                            last = pe.matmul(mlp_ps[:, m, :], w2_sb[:, c, m * P:(m + 1) * P], a1[:, c, :],
                                             start=(c == 0), stop=(c == M1 - 1))
                else:
                    pe.wait_ge(mlp_act, done + 8)
                    for c in range(M2):
                        last = pe.matmul(mlp_ps[0:1, 0, :], w3_sb[:, c:c + 1], a2[:, c, :],
                                         start=(c == 0), stop=(c == M2 - 1))
                last.then_inc(mlp_mm, 1)

            pe.wait_ge(constants, 6)
            pe.wait_ge(identity_rounded, 1)
            transpose_group(Step(0, 0, 0, first=True), 0)
            pe.wait_ge(low_weights, PIECES)
            pe.wait_ge(high_weights, PIECES)
            pe.wait_ge(dense_in, 16 * (OCTET + GROUP))
            pe.wait_ge(params_in, 8 * 16)

            def emit(b):
                for j in range(FIELDS):
                    if j in MLP_AT and not b.first:
                        mlp_waits(b.before(), MLP_AT[j])
                    for g in range(1, GROUPS):
                        if FRONT_AT[g] == j:
                            transpose_group(b, g)
                    if j == FRONT_AT[0] and not b.last:
                        transpose_group(b.after(), 0)
                    for i in range(TILES_BEFORE[j], TILES_BEFORE[j + 1]):
                        interact(b, i)
                        if i == TILES_BEFORE[j] and j in MLP_AT and not b.first:
                            mlp(b.before(), MLP_AT[j])
                        if i >= CONTRACT_LAG:
                            contract(b, i - CONTRACT_LAG)
                        elif not b.first:
                            contract(b.before(), NT + i - CONTRACT_LAG)

            each_block(pe, emit)
            final = Step(BLOCKS - 1, BLOCKS // 2 - 1, 1)
            for i in range(NT - CONTRACT_LAG, NT):
                contract(final, i)
            for stage in MLP_AT.values():
                mlp_waits(final, stage)
                mlp(final, stage)


def layouts(w, dense_w):
    import numpy as np

    pair = {}
    for i in range(FIELDS):
        for j in range(i + 1, FIELDS):
            pair[i, j] = len(pair)
    w_units = np.zeros((E, UNITS, P), w.dtype)
    dw_doubles = np.zeros((OCTET, DOUBLES, D), dense_w.dtype)
    dw_singles = np.zeros((GROUP, SINGLES, D), dense_w.dtype)
    half_rows = E // 2
    for j in range(FIELDS):
        doubles, single = field_units(j)
        for d in range(doubles):
            for s in range(OCTET):
                i = OCTET * d + s
                if i < j:
                    for h in range(2):
                        w_units[:, UNIT_AT[j] + 2 * d + h, s * half_rows:(s + 1) * half_rows] = \
                            w[pair[i, j]][h::2, :].T
                    dw_doubles[s, DOUBLE_AT[j] + d] = dense_w[pair[i, j]]
        if single:
            for s in range(GROUP):
                i = OCTET * (j // OCTET) + s
                if i < j:
                    w_units[:, UNIT_AT[j] + 2 * doubles, s * E:(s + 1) * E] = w[pair[i, j]].T
                    dw_singles[s, SINGLE_AT[j]] = dense_w[pair[i, j]]
    return w_units.reshape(E, UNITS * P), dw_doubles, dw_singles


def by_partition(v):
    import numpy as np

    return np.asarray(v).reshape(-1, P).T


def kernel(**inputs):
    import numpy as np
    import concourse.bacc as bacc
    from concourse.bass_utils import run_bass_kernel_spmd

    w_units, dw_doubles, dw_singles = layouts(np.asarray(inputs["L0_rec_W"]), np.asarray(inputs["L0_rec_dense_w"]))
    arrays = {"ids": inputs["ids"]}
    for f in range(FIELDS):
        arrays[f"tbl_{f}"] = inputs[f"tbl_{f}"]
    arrays.update(
        w_units=w_units, dw_doubles=dw_doubles, dw_singles=dw_singles,
        dense_b=inputs["L0_rec_dense_b"], gamma=inputs["L0_rec_gamma"], beta=inputs["L0_rec_beta"],
        ctx_t=np.asarray(inputs["dense_ctx"]).T, w1=inputs["W_top1"], b1=by_partition(inputs["b_top1"]),
        w2=inputs["W_top2"], b2=by_partition(inputs["b_top2"]), w3=by_partition(inputs["W_top3"]))
    arrays = {name: np.ascontiguousarray(a) for name, a in arrays.items()}
    nc = bacc.Bacc("TRN2", target_bir_lowering=False, num_devices=1)
    aps = {name: nc.dram_tensor(f"in_{name}", a.shape, mybir.dt.from_np(a.dtype), kind="ExternalInput").ap()
           for name, a in arrays.items()}
    out = nc.dram_tensor("out", (arrays["ids"].shape[0], 1), F32, kind="ExternalOutput").ap()
    tables = [aps.pop(f"tbl_{f}") for f in range(FIELDS)]
    interaction_tower(nc, tables=tables, out=out, **aps)
    result = run_bass_kernel_spmd(nc, [{f"in_{name}": a for name, a in arrays.items()}], core_ids=[0])
    return result.results[0]["out"]
```

```python
import concourse.bass as bass
from concourse import mybir
from contextlib import ExitStack

F32 = mybir.dt.float32
F32R = mybir.dt.float32r
I32 = mybir.dt.int32
ALU = mybir.AluOpType
ACT = mybir.ActivationFunctionType

P = 128
FIELDS = 40
E = 32
GROUP = 4
GROUPS = FIELDS // GROUP
D = 16
QUADS = 4
LN_EPS = 1e-3
BS = 256
BT = BS // P


def plan():
    tiles = []
    for g in range(GROUPS):
        left = []
        for j in range(GROUP * g, GROUP * (g + 1)):
            n = g + (j > GROUP * g)
            tiles += [[(j, w, TILE_UNITS)] for w in range(0, n - n % TILE_UNITS, TILE_UNITS)]
            if n % TILE_UNITS:
                seg = (j, n - n % TILE_UNITS, n % TILE_UNITS)
                if left and (left[-1][1:] != seg[1:] or (len(left) + 1) * seg[2] > TILE_UNITS):
                    tiles.append(left)
                    left = []
                left = left + [seg]
        tiles += [left] * bool(left)
    return tiles


TILE_UNITS = 4
TILES = plan()
NT = len(TILES)
RING = 3
assert NT % 2 == 0 and NT % RING == 0
TILES_BEFORE = [sum(tile[0][0] < GROUP * g for tile in TILES) for g in range(GROUPS + 1)]
GROUP_OF = [tile[0][0] // GROUP for tile in TILES]
UNITS_IN = [sum(seg[2] for seg in tile) for tile in TILES]
UNITS_BEFORE = [sum(UNITS_IN[:i]) for i in range(NT + 1)]
UNITS = UNITS_BEFORE[NT]

PIECES = 21
PIECE = UNITS // PIECES * P
assert UNITS % PIECES == 0

CONTRACT_LAG = 3


def inside(g, share):
    return TILES_BEFORE[g] + int(share * (TILES_BEFORE[g + 1] - TILES_BEFORE[g] - 1))


SPLIT_AFTER = {inside(g, 0.3): (g + 1) % GROUPS for g in range(GROUPS)}
FRONT_AFTER = {inside(g, 0.6): (g + 1) % GROUPS for g in range(GROUPS)}
FIRST_SPLIT_PIECE = 6
COPY_H_AFTER = CONTRACT_LAG - 1
MLP_AFTER = {20: "center", 23: "variance", 28: "up_low", 30: "up_high", 33: "middle_0", 34: "middle_1",
             36: "middle_2", 37: "middle_3", 41: "out"}
MLP_NORM_AFTER = 25
STORED_AFTER = 55
MLP_STAGES = len(MLP_AFTER)
XS_RING = 5


def interaction_tower(nc, ids, tables, w_units, dw, dense_b, gamma, beta, ctx_t,
                      w1, b1, w2, b2, w3, out):
    B = ids.shape[0]
    BLOCKS = B // BS
    H1, H2 = w2.shape
    M1, M2 = H1 // P, H2 // P
    C = w1.shape[0]
    assert BLOCKS >= 4 and BLOCKS % 2 == 0 and M1 == 4 and M2 == 2

    with ExitStack() as ctx:
        def sb(name, shape, dt=F32):
            return ctx.enter_context(nc.sbuf_tensor(name, shape, dt))

        def sem(name):
            return ctx.enter_context(nc.semaphore(name))

        w_split = sb("w_split", [P, UNITS * P], F32R)
        dw_sb = sb("dw_sb", [P, UNITS, D])
        windows = sb("windows", [P, 2, GROUPS, BS])
        movers = sb("movers", [P, 2, GROUP, BS], F32R)
        x_nat = sb("x_nat", [P, GROUPS, BT, GROUP * E])
        x_split = sb("x_split", [P, XS_RING, BT, GROUP, 2, E], F32R)
        products = sb("products", [P, RING, TILE_UNITS, BS])
        ids_sb = sb("ids_sb", [P, 2, BT, FIELDS], I32)
        identity = sb("identity", [P, P])
        identity_r = sb("identity_r", [P, P], F32R)
        centering = sb("centering", [P, D])
        averaging = sb("averaging", [D, D])
        db_sb, gamma_sb, beta_sb = sb("db_sb", [P, 1]), sb("gamma_sb", [D, 1]), sb("beta_sb", [D, 1])
        w1_sb = sb("w1_sb", [C, H1])
        w2_sb = sb("w2_sb", [P, M1, H2])
        w3_sb = sb("w3_sb", [P, M2])
        b1_sb, b2_sb = sb("b1_sb", [P, M1]), sb("b2_sb", [P, M2])
        h_sb = sb("h_sb", [P, BS])
        hc_sb, sq_sb, std_sb = sb("hc_sb", [D, BS]), sb("sq_sb", [D, BS]), sb("std_sb", [D, BS])
        rstd_sb = sq_sb
        eps_sb = sb("eps_sb", [D, 1])
        z_cat = sb("z_cat", [C, 2, BS])
        a1 = sb("a1", [P, M1, BS])
        a2 = a1[:, 0:M2, :]
        y_sb = sb("y_sb", [1, BS])
        flats = [windows[0:64, 1, :, :].rearrange("p u b -> p (u b)"),
                 products[0:64, :, :, :].rearrange("p r u b -> p (r u b)")]
        staging = [flat[:, s * PIECE:(s + 1) * PIECE]
                   for flat, size in zip(flats, (GROUPS * BS, RING * TILE_UNITS * BS))
                   for s in range(size // PIECE)]
        STAGES = len(staging)

        t_ps = ctx.enter_context(nc.psum_tensor("t_ps", [P, 2, TILE_UNITS, BS], F32))
        mover_ps = ctx.enter_context(nc.psum_tensor("mover_ps", [P, 2, BS], F32))
        window_ps = ctx.enter_context(nc.psum_tensor("window_ps", [P, 2 * BS], F32))
        h_ps = ctx.enter_context(nc.psum_tensor("h_ps", [P, 2 * BS], F32))
        mlp_ps = ctx.enter_context(nc.psum_tensor("mlp_ps", [P, 2, BS], F32))

        weights_in = [sem(f"weights_in{s}") for s in range(len(staging))]
        dense_in = sem("dense_in")
        params_in = sem("params_in")
        ids_in = [sem(f"ids_in{s}") for s in range(2)]
        context_in = [sem(f"context_in{s}") for s in range(2)]
        gathered = [sem(f"gathered{g}") for g in range(GROUPS)]
        high_weights = sem("high_weights")
        low_weights = sem("low_weights")
        constants = sem("constants")
        identity_rounded = sem("identity_rounded")
        high_split = sem("high_split")
        low_split = sem("low_split")
        h_cleared = sem("h_cleared")
        movers_transposed = sem("movers_transposed")
        windows_transposed = sem("windows_transposed")
        movers_ready = sem("movers_ready")
        windows_ready = sem("windows_ready")
        t_ready = sem("t_ready")
        multiplied = sem("multiplied")
        contracted = sem("contracted")
        h_copied = sem("h_copied")
        mlp_mm = sem("mlp_mm")
        mlp_act = sem("mlp_act")
        normed = sem("normed")
        out_done = sem("out_done")

        block = ctx.enter_context(nc.Block())

        class Step:

            def __init__(self, k, half, parity, first=False, last=False):
                self.k, self.half, self.parity, self.first, self.last = k, half, parity, first, last

            def before(self):
                return Step(self.k - 1, self.half - (1 - self.parity), 1 - self.parity)

            def after(self):
                return Step(self.k + 1, self.half + self.parity, 1 - self.parity)

        def each_block(engine, emit):
            emit(Step(0, 0, 0, first=True))
            with engine.Fori(0, BLOCKS // 2 - 1) as i:
                emit(Step(2 * i + 1, i, 1))
                emit(Step(2 * i + 2, i + 1, 0))
            emit(Step(BLOCKS - 1, BLOCKS // 2 - 1, 1, last=True))

        ACT_STEPS = 9
        NORM_STEPS = 3

        @block.sync
        def _(sp):
            for piece in range(PIECES):
                s = piece % STAGES
                if piece >= STAGES:
                    sp.wait_ge(high_weights, piece - STAGES + 1)
                    sp.wait_ge(low_weights, piece - STAGES + 1)
                for copy in range(2):
                    sp.dma_start(staging[s][copy * E:(copy + 1) * E, :],
                                 w_units[:, piece * PIECE:(piece + 1) * PIECE]).then_inc(weights_in[s], 16)

        @block.gpsimd
        def _(pool):
            pool.memset(identity[:], 0.0).then_inc(constants, 1)
            pool.memset(centering[:], -1.0 / D).then_inc(constants, 1)
            pool.memset(averaging[:], 1.0 / D).then_inc(constants, 1)
            pool.memset(eps_sb[:], LN_EPS).then_inc(constants, 1)
            to_be_read = [pool.alloc_register(f"to_be_read{s}") for s in range(2)]
            pool.reg_mov(to_be_read[0], 1)

            def finish_constants():
                pool.wait_ge(constants, 4)
                pool.affine_select(out=identity[:], in_=identity[:], compare_op=ALU.not_equal, fill=1.0,
                                   base=0, pattern=[[-1, P]], channel_multiplier=1).then_inc(constants, 1)
                for q in range(QUADS):
                    pool.affine_select(out=centering[:], in_=centering[:], compare_op=ALU.not_equal,
                                       fill=1.0 - 1.0 / D, base=-32 * q, pattern=[[-1, D]],
                                       channel_multiplier=1).then_inc(constants, 1)
                    pool.wait_ge(constants, 6 + q)

            def gather(b, g):
                if g == 0:
                    pool.wait_ge(ids_in[b.parity], 16 * (b.half + 1))
                if not b.first:
                    count = GROUPS * (b.k - 1) + g + 1 if b.last else to_be_read[g % 2]
                    pool.wait_ge(low_split, count)
                    pool.wait_ge(windows_transposed, count)
                    if not b.last:
                        pool.reg_add(to_be_read[(g + 1) % 2], to_be_read[g % 2], 1)
                for t in range(BT):
                    for f in range(GROUP):
                        field = GROUP * g + f
                        pool.indirect_dma_start(
                            x_nat[:, g, t, f * E:(f + 1) * E], None, tables[field][:, :],
                            bass.IndirectOffsetOnAxis(ap=ids_sb[:, b.parity, t, field:field + 1], axis=0)
                        ).then_inc(gathered[g], 16)

            def emit(b):
                for g in range(GROUPS):
                    gather(b, g)
                    if b.first and g == 0:
                        finish_constants()

            each_block(pool, emit)

        @block.scalar
        def _(act):
            def load_ids(b):
                act.dma_start(ids_sb[:, b.parity, :, :],
                              ids[bass.ds(b.k * BS, BS), :].rearrange("(t p) f -> p t f", p=P)
                              ).then_inc(ids_in[b.parity], 16)

            def load_context(b):
                act.dma_start(z_cat[D:C, b.parity, :], ctx_t[:, bass.ds(b.k * BS, BS)]
                              ).then_inc(context_in[b.parity], 16)

            load_ids(Step(0, 0, 0))
            for dst, src in ((db_sb, dense_b), (gamma_sb, gamma), (beta_sb, beta)):
                if dst is db_sb:
                    act.wait_ge(h_cleared, 2)
                act.dma_start(dst[0:D, :], src.rearrange("(d o) -> d o", o=1)).then_inc(params_in, 16)
            for s in range(GROUP):
                act.dma_start(dw_sb[s * E:(s + 1) * E, :, :], dw[s:s + 1, :, :].broadcast_to([E, UNITS, D])
                              ).then_inc(dense_in, 16)
            act.dma_start(w1_sb[:, :], w1).then_inc(params_in, 16)
            act.dma_start(w2_sb[:, :, :], w2.rearrange("(m p) n -> p m n", p=P)).then_inc(params_in, 16)
            act.dma_start(w3_sb[:, :], w3).then_inc(params_in, 16)
            act.dma_start(b1_sb[:, :], b1).then_inc(params_in, 16)
            act.dma_start(b2_sb[:, :], b2).then_inc(params_in, 16)

            def split_high(b, g):
                act.wait_ge(gathered[g], BT * GROUP * 16 * (b.k + 1))
                if not b.first or g >= XS_RING:
                    act.wait_ge(movers_transposed, GROUPS * b.k + g - XS_RING + 1)
                xs = x_split[:, g % XS_RING, :, :, :, :]
                act.activation(xs[:, :, :, 0, :],
                               x_nat[:, g, :, :].rearrange("p t (f e) -> p t f e", e=E),
                               ACT.Copy).then_inc(high_split, 1)

            def evacuate(b, g):
                seq = GROUPS * b.k + g
                act.wait_ge(movers_transposed, seq + 1)
                if not b.first or g >= 2:
                    behind = b if g >= 2 else b.before()
                    act.wait_ge(t_ready, NT * behind.k + TILES_BEFORE[(g - 2) % GROUPS + 1])
                slot = movers[:, g % 2, :, :].rearrange("p (a c) b -> p a c b", c=2)
                for odd in range(2):
                    for half in range(2):
                        last = act.activation(slot[half * 64:(half + 1) * 64, :, odd, :],
                                              mover_ps[odd * 64:(odd + 1) * 64, :, :], ACT.Copy)
                last.then_inc(movers_ready, 1)
                act.wait_ge(windows_transposed, seq + 1)
                if g == 0 and not b.first:
                    act.wait_ge(multiplied, NT * (b.k - 1) + 1)
                act.activation(windows[:, b.parity, g, :], window_ps[:, 0:BS], ACT.Copy).then_inc(windows_ready, 1)

            def mlp(b, stage):
                stage_no = list(MLP_AFTER.values()).index(stage)
                act.wait_ge(mlp_mm, MLP_STAGES * b.k + stage_no + 1)
                done = ACT_STEPS * b.k
                if stage == "center":
                    act.activation(sq_sb[:, :], mlp_ps[0:D, 0, :], ACT.Square).then_inc(mlp_act, 1)
                    act.activation(hc_sb[:, :], mlp_ps[0:D, 0, :], ACT.Copy).then_inc(mlp_act, 1)
                elif stage == "variance":
                    act.activation(std_sb[:, :], mlp_ps[0:D, 0, :], ACT.Sqrt, bias=eps_sb[:, :]
                                   ).then_inc(mlp_act, 1)
                elif stage in ("up_low", "up_high"):
                    for m in range(2):
                        c = 2 * (stage == "up_high") + m
                        act.activation(a1[:, c, :], mlp_ps[:, m, :], ACT.Relu, bias=b1_sb[:, c:c + 1]
                                       ).then_inc(mlp_act, 1)
                elif stage == "middle_3":
                    for m in range(2):
                        last = act.activation(a2[:, m, :], mlp_ps[:, m, :], ACT.Relu,
                                              bias=b2_sb[:, m:m + 1])
                    last.then_inc(mlp_act, 1)
                elif stage == "out":
                    act.activation(y_sb[:, :], mlp_ps[0:1, 0, :], ACT.Copy).then_inc(mlp_act, 1)
                    act.wait_ge(mlp_act, done + ACT_STEPS)
                    act.dma_start(out[bass.ds(b.k * BS, BS), :].rearrange("b o -> o b"), y_sb[:, :]
                                  ).then_inc(out_done, 16)

            def copy_h(b):
                act.wait_ge(contracted, NT * (b.k + 1))
                act.activation(h_sb[:, :], h_ps[:, 0:BS], ACT.Identity,
                               bias=db_sb[:, :]).then_inc(h_copied, 1)

            act.wait_ge(constants, 9)
            act.activation(identity_r[:, :], identity[:, :], ACT.Copy).then_inc(identity_rounded, 1)
            for piece in range(PIECES):
                s = piece % STAGES
                act.wait_ge(weights_in[s], 32 * (piece // STAGES + 1))
                act.activation(w_split[0:64, piece * PIECE:(piece + 1) * PIECE], staging[s][:, :], ACT.Copy
                               ).then_inc(high_weights, 1)
                if piece == FIRST_SPLIT_PIECE:
                    split_high(Step(0, 0, 0, first=True), 0)
            evacuate(Step(0, 0, 0, first=True), 0)
            act.wait_ge(params_in, 8 * 16)

            def emit(b):
                if not b.last:
                    load_ids(b.after())
                load_context(b)
                for i in range(NT):
                    if i == COPY_H_AFTER and not b.first:
                        copy_h(b.before())
                    if i in MLP_AFTER and not b.first:
                        mlp(b.before(), MLP_AFTER[i])
                    if i == STORED_AFTER and not b.first:
                        act.wait_ge(out_done, 16 * b.k)
                    for events, do in ((SPLIT_AFTER, split_high), (FRONT_AFTER, evacuate)):
                        if i in events and (events[i] > 0 or not b.last):
                            do(b if events[i] > 0 else b.after(), events[i])

            each_block(act, emit)
            final = Step(BLOCKS - 1, BLOCKS // 2 - 1, 1)
            copy_h(final)
            for stage in MLP_AFTER.values():
                mlp(final, stage)
            act.wait_ge(out_done, 16 * BLOCKS)

        @block.vector
        def _(dve):
            dve.memset(h_ps[:, :], 0.0).then_inc(h_cleared, 1)
            dve.memset(db_sb[:, :], 0.0).then_inc(h_cleared, 1)

            def split_low(b, g):
                dve.wait_ge(high_split, GROUPS * b.k + g + 1)
                dve.wait_ge(gathered[g], BT * GROUP * 16 * (b.k + 1))
                xs = x_split[:, g % XS_RING, :, :, :, :]
                dve.tensor_tensor(xs[:, :, :, 1, :], x_nat[:, g, :, :].rearrange("p t (f e) -> p t f e", e=E),
                                  xs[:, :, :, 0, :].bitcast(F32), ALU.subtract).then_inc(low_split, 1)

            for piece in range(PIECES):
                s = piece % STAGES
                dve.wait_ge(weights_in[s], 32 * (piece // STAGES + 1))
                dve.wait_ge(high_weights, piece + 1)
                at = slice(piece * PIECE, (piece + 1) * PIECE)
                dve.tensor_tensor(w_split[64:P, at], staging[s][:, :], w_split[0:64, at].bitcast(F32),
                                  ALU.subtract).then_inc(low_weights, 1)
                if piece == FIRST_SPLIT_PIECE:
                    split_low(Step(0, 0, 0, first=True), 0)
            dve.wait_ge(params_in, 8 * 16)

            def multiply(b, i):
                n = NT * b.k + i
                dve.wait_ge(t_ready, n + 1)
                if TILES_BEFORE[GROUP_OF[i]] == i:
                    dve.wait_ge(windows_ready, GROUPS * b.k + GROUP_OF[i] + 1)
                if not b.first or i >= RING:
                    dve.wait_ge(contracted, n + 1 - RING)
                segments = len(TILES[i])
                _, w, count = TILES[i][0]
                window = windows[:, b.parity, w:w + count, :].rearrange("p u b -> p (u b)")
                dst = products[:, i % RING, 0:UNITS_IN[i], :].rearrange("p (s u) b -> p s (u b)", s=segments)
                t = t_ps[:, i % 2, 0:UNITS_IN[i], :].rearrange("p (s u) b -> p s (u b)", s=segments)
                window = window.unsqueeze(1).broadcast_to([P, segments, count * BS])
                dve.tensor_tensor(dst, t, window, ALU.mult).then_inc(multiplied, 1)

            def norm(b):
                dve.wait_ge(mlp_act, ACT_STEPS * b.k + 3)
                dve.reciprocal(rstd_sb[:, :], std_sb[:, :]).then_inc(normed, 1)
                dve.wait_ge(normed, NORM_STEPS * b.k + 1)
                dve.tensor_tensor(rstd_sb[:, :], hc_sb[:, :], rstd_sb[:, :], ALU.mult).then_inc(normed, 1)
                dve.wait_ge(normed, NORM_STEPS * b.k + 2)
                dve.tensor_scalar(z_cat[0:D, b.parity, :], rstd_sb[:, :], gamma_sb[:, :], beta_sb[:, :],
                                  ALU.mult, ALU.add).then_inc(normed, 1)

            def emit(b):
                for i in range(NT):
                    multiply(b, i)
                    if i == MLP_NORM_AFTER and not b.first:
                        norm(b.before())
                    if i in SPLIT_AFTER and (SPLIT_AFTER[i] > 0 or not b.last):
                        split_low(b if SPLIT_AFTER[i] > 0 else b.after(), SPLIT_AFTER[i])

            each_block(dve, emit)
            norm(Step(BLOCKS - 1, BLOCKS // 2 - 1, 1))

        @block.tensor
        def _(pe):
            def transpose_group(b, g):
                seq = GROUPS * b.k + g
                pe.wait_ge(low_split, seq + 1)
                if not b.first or g >= 1:
                    pe.wait_ge(movers_ready, seq)
                for pair in range(2):
                    for t in range(BT):
                        last = pe.matmul(
                            mover_ps[:, pair, t * P:(t + 1) * P],
                            x_split[:, g % XS_RING, t, 2 * pair:2 * pair + 2, :, :].rearrange("p f h e -> p (f h e)"),
                            identity_r[:, :], start=True, stop=True)
                last.then_inc(movers_transposed, 1)
                if not b.first or g >= 1:
                    pe.wait_ge(windows_ready, seq)
                pe.wait_ge(gathered[g], BT * GROUP * 16 * (b.k + 1))
                for t in range(BT):
                    last = pe.transpose(window_ps[:, t * P:(t + 1) * P], x_nat[:, g, t, :], identity[:, :])
                last.then_inc(windows_transposed, 1)

            def interact(b, i):
                n = NT * b.k + i
                if TILES_BEFORE[GROUP_OF[i]] == i:
                    pe.wait_ge(movers_ready, GROUPS * b.k + GROUP_OF[i] + 1)
                if not isinstance(n, int) or n >= 2:
                    pe.wait_ge(multiplied, n - 1)
                at = 0
                for j, _, count in TILES[i]:
                    for _ in range(count):
                        u = UNITS_BEFORE[i] + at
                        last = pe.matmul(t_ps[:, i % 2, at, :], w_split[:, u * P:(u + 1) * P],
                                         movers[:, j // GROUP % 2, j % GROUP, :], start=True, stop=True)
                        at += 1
                last.then_inc(t_ready, 1)

            def contract(b, i):
                pe.wait_ge(multiplied, NT * b.k + i + 1)
                if i == 0 and not b.first:
                    pe.wait_ge(h_copied, b.k)
                for at in range(UNITS_IN[i]):
                    u = UNITS_BEFORE[i] + at
                    q = u % QUADS
                    last = pe.matmul(h_ps[32 * q:32 * q + D, 0:BS], dw_sb[:, u, :], products[:, i % RING, at, :],
                                     start=(u < QUADS), stop=(u >= UNITS - QUADS))
                last.then_inc(contracted, 1)

            def mlp_waits(b, stage):
                done = ACT_STEPS * b.k
                if stage == "center":
                    pe.wait_ge(h_copied, b.k + 1)
                elif stage == "variance":
                    pe.wait_ge(mlp_act, done + 2)

            def mlp(b, stage):
                done = ACT_STEPS * b.k
                if stage == "center":
                    last = pe.matmul(mlp_ps[0:D, 0, :], centering[:, :], h_sb[:, :], start=True, stop=True)
                elif stage == "variance":
                    last = pe.matmul(mlp_ps[0:D, 0, :], averaging[:, :], sq_sb[:, :], start=True, stop=True)
                elif stage in ("up_low", "up_high"):
                    if stage == "up_low":
                        pe.wait_ge(mlp_act, done + 3)
                        pe.wait_ge(normed, NORM_STEPS * (b.k + 1))
                        pe.wait_ge(context_in[b.parity], 16 * (b.half + 1))
                    else:
                        pe.wait_ge(mlp_act, done + 5)
                    for m in range(2):
                        c = 2 * (stage == "up_high") + m
                        last = pe.matmul(mlp_ps[:, m, :], w1_sb[:, c * P:(c + 1) * P], z_cat[:, b.parity, :],
                                         start=True, stop=True)
                elif stage != "out":
                    quarter = int(stage[-1])
                    if quarter == 0:
                        pe.wait_ge(mlp_act, done + 7)
                    m = quarter // 2
                    for c in range(quarter % 2 * 2, quarter % 2 * 2 + 2):
                        last = pe.matmul(mlp_ps[:, m, :], w2_sb[:, c, m * P:(m + 1) * P], a1[:, c, :],
                                         start=(c == 0), stop=(c == M1 - 1))
                else:
                    pe.wait_ge(mlp_act, done + 8)
                    for c in range(M2):
                        last = pe.matmul(mlp_ps[0:1, 0, :], w3_sb[:, c:c + 1], a2[:, c, :],
                                         start=(c == 0), stop=(c == M2 - 1))
                last.then_inc(mlp_mm, 1)

            pe.wait_ge(constants, 9)
            pe.wait_ge(identity_rounded, 1)
            transpose_group(Step(0, 0, 0, first=True), 0)
            pe.wait_ge(low_weights, PIECES)
            pe.wait_ge(high_weights, PIECES)
            pe.wait_ge(dense_in, 16 * GROUP)
            pe.wait_ge(h_cleared, 1)
            pe.wait_ge(params_in, 8 * 16)

            def emit(b):
                for i in range(NT):
                    stage = None if b.first else MLP_AFTER.get(i)
                    if stage:
                        mlp_waits(b.before(), stage)
                    if i >= CONTRACT_LAG:
                        contract(b, i - CONTRACT_LAG)
                    elif not b.first:
                        contract(b.before(), NT + i - CONTRACT_LAG)
                    if stage:
                        mlp(b.before(), stage)
                    interact(b, i)
                    if i in FRONT_AFTER and (FRONT_AFTER[i] > 0 or not b.last):
                        transpose_group(b if FRONT_AFTER[i] > 0 else b.after(), FRONT_AFTER[i])

            each_block(pe, emit)
            final = Step(BLOCKS - 1, BLOCKS // 2 - 1, 1)
            for i in range(NT - CONTRACT_LAG, NT):
                contract(final, i)
            for stage in MLP_AFTER.values():
                mlp_waits(final, stage)
                mlp(final, stage)


def layouts(w, dense_w):
    import numpy as np

    pair = {}
    for i in range(FIELDS):
        for j in range(i + 1, FIELDS):
            pair[i, j] = len(pair)
    w_units = np.zeros((E, UNITS, P), w.dtype)
    dw = np.zeros((GROUP, UNITS, D), dense_w.dtype)
    order = [(j, first + n) for tile in TILES for j, first, count in tile for n in range(count)]
    for u, (j, window) in enumerate(order):
        for s in range(GROUP):
            i = GROUP * window + s
            if i < j:
                w_units[:, u, s * E:(s + 1) * E] = w[pair[i, j]].T
                dw[s, u] = dense_w[pair[i, j]]
    return w_units.reshape(E, UNITS * P), dw


def by_partition(v):
    import numpy as np

    return np.asarray(v).reshape(-1, P).T


def kernel(**inputs):
    import numpy as np
    import concourse.bacc as bacc
    from concourse.bass_utils import run_bass_kernel_spmd

    w_units, dw = layouts(np.asarray(inputs["L0_rec_W"]), np.asarray(inputs["L0_rec_dense_w"]))
    arrays = {"ids": inputs["ids"]}
    for f in range(FIELDS):
        arrays[f"tbl_{f}"] = inputs[f"tbl_{f}"]
    arrays.update(
        w_units=w_units, dw=dw,
        dense_b=inputs["L0_rec_dense_b"], gamma=inputs["L0_rec_gamma"], beta=inputs["L0_rec_beta"],
        ctx_t=np.asarray(inputs["dense_ctx"]).T, w1=inputs["W_top1"], b1=by_partition(inputs["b_top1"]),
        w2=inputs["W_top2"], b2=by_partition(inputs["b_top2"]), w3=by_partition(inputs["W_top3"]))
    arrays = {name: np.ascontiguousarray(a) for name, a in arrays.items()}
    nc = bacc.Bacc("TRN2", target_bir_lowering=False, num_devices=1)
    aps = {name: nc.dram_tensor(f"in_{name}", a.shape, mybir.dt.from_np(a.dtype), kind="ExternalInput").ap()
           for name, a in arrays.items()}
    out = nc.dram_tensor("out", (arrays["ids"].shape[0], 1), F32, kind="ExternalOutput").ap()
    tables = [aps.pop(f"tbl_{f}") for f in range(FIELDS)]
    interaction_tower(nc, tables=tables, out=out, **aps)
    result = run_bass_kernel_spmd(nc, [{f"in_{name}": a for name, a in arrays.items()}], core_ids=[0])
    return result.results[0]["out"]
```

```python
import concourse.bass as bass
from concourse import mybir
from contextlib import ExitStack

F32 = mybir.dt.float32
F32R = mybir.dt.float32r
I32 = mybir.dt.int32
ALU = mybir.AluOpType
ACT = mybir.ActivationFunctionType

P = 128
FIELDS = 40
E = 32
GROUP = 4
GROUPS = FIELDS // GROUP
D = 16
QUADS = 4
QUAD = 32
LN_EPS = 1e-3
BS = 256
BT = BS // P

TILES = [(g, w) for g in range(GROUPS) for w in range(g + 1)]
NT = len(TILES)
TILE_MOVERS = [range(GROUP * g + (w == g), GROUP * (g + 1)) for g, w in TILES]
RING = 5
assert NT % RING == 0
TILES_BEFORE = [g * (g + 1) // 2 for g in range(GROUPS + 1)]
UNITS_IN = [len(movers) for movers in TILE_MOVERS]
UNITS_BEFORE = [sum(UNITS_IN[:i]) for i in range(NT + 1)]
UNITS = UNITS_BEFORE[NT]

PIECES = 21
PIECE = UNITS // PIECES * P
assert UNITS % PIECES == 0

HOT = (3, 27)
HOT_CHUNKS = 8
HOT_LEAD = (GROUP - 1) * E
HOT_GROUPS = [f // GROUP for f in HOT]
assert len(HOT) == 2 and all(f % GROUP == GROUP - 1 for f in HOT)
HOT_LOAD_AFTER = (20, 0)
HOT_AFTER = (25, 4)
HOT_PARTS_AFTER = ((46, 47, 48, 49), (15, 16, 17, 18))
HOT_PARTS = len(HOT_PARTS_AFTER[0])

CONTRACT_LAG = 3
XS_RING = 2
MOVERS_RING = 4

SPLIT_AFTER = {49: 0, 51: 1, 53: 2, 2: 3, 6: 4, 11: 5, 17: 6, 23: 7, 30: 8, 39: 9}
FRONT_AFTER = {51: 0, 53: 1, 0: 2, 4: 3, 8: 4, 13: 5, 19: 6, 25: 7, 32: 8, 41: 9}
PIECES_BEFORE = (14, 4, 3)
assert len(PIECES_BEFORE) == sum(g < TILES[i][0] for i, g in SPLIT_AFTER.items())
assert sum(PIECES_BEFORE) == PIECES
FRONTS_FIRST = sum(g < TILES[i][0] for i, g in FRONT_AFTER.items())
PIECES_ALONE = 5
HIGH_FIRST = 3

COPY_H_AFTER = CONTRACT_LAG - 1
MLP_AFTER = {6: "center", 10: "variance", 17: "up_0", 19: "up_1", 21: "up_2", 23: "up_3"}
MLP_AFTER.update({26 + 2 * c: f"middle_{c}" for c in range(8)})
MLP_AFTER[44] = "out"
MLP_NORM_AFTER = 13
STORED_AFTER = 50
MLP_STAGES = len(MLP_AFTER)


def plain_fields(g):
    return GROUP - 1 if g in HOT_GROUPS else GROUP


def interaction_tower(nc, ids, hot_ids, hot_rows, tables, w_units, dw, dense_b, gamma, beta, ctx_t,
                      w1, b1, w2, b2, w3, out):
    B = ids.shape[0]
    BLOCKS = B // BS
    H1, H2 = w2.shape
    M1, M2 = H1 // P, H2 // P
    C = w1.shape[0]
    HOT_ROWS = tables[HOT[0]].shape[0] // HOT_CHUNKS
    assert all(tables[f].shape[0] == HOT_ROWS * HOT_CHUNKS for f in HOT) and HOT_ROWS <= P
    assert BLOCKS >= 4 and BLOCKS % 2 == 0 and M1 == 4 and M2 == 2

    with ExitStack() as ctx:
        def sb(name, shape, dt=F32):
            return ctx.enter_context(nc.sbuf_tensor(name, shape, dt))

        def sem(name):
            return ctx.enter_context(nc.semaphore(name))

        w_split = sb("w_split", [P, UNITS * P], F32R)
        dw_sb = sb("dw_sb", [P, UNITS, D])
        windows = sb("windows", [P, GROUPS, BS])
        movers = sb("movers", [P, MOVERS_RING, GROUP, BS], F32R)
        x_nat = sb("x_nat", [P, GROUPS, BT, GROUP * E])
        x_split = sb("x_split", [P, XS_RING, BT, GROUP, 2, E], F32R)
        hot_flat = sb("hot_flat", [HOT_ROWS, HOT_LEAD + len(HOT) * HOT_CHUNKS * 2 * E], F32R)
        hot_split = hot_flat[:, HOT_LEAD:].rearrange("p (c h e) -> p c h e", h=2, e=E)
        hot_rows_sb = sb("hot_rows_sb", [HOT_ROWS, HOT_CHUNKS])
        hot_ids_sb = sb("hot_ids_sb", [HOT_ROWS, BS], I32)
        hot_ids_f = hot_ids_sb[:, :].bitcast(F32)
        one_hot = sb("one_hot", [HOT_ROWS, HOT_CHUNKS, BS], F32R)
        products = sb("products", [P, RING, GROUP, BS])
        ids_sb = sb("ids_sb", [P, 2, BT, FIELDS], I32)
        identity = sb("identity", [P, P])
        identity_r = sb("identity_r", [P, P], F32R)
        centering = sb("centering", [P, QUAD])
        averaging = sb("averaging", [P, P])
        db_sb, gamma_sb, beta_sb = sb("db_sb", [P, 1]), sb("gamma_sb", [P, 1]), sb("beta_sb", [P, 1])
        w1_sb = sb("w1_sb", [C, H1])
        w2_sb = sb("w2_sb", [P, M1, H2])
        w3_sb = sb("w3_sb", [P, M2])
        b1_sb, b2_sb = sb("b1_sb", [P, M1]), sb("b2_sb", [P, M2])
        h_sb = sb("h_sb", [P, BS])
        sq_sb, std_sb = sb("sq_sb", [P, BS // QUADS]), sb("std_sb", [P, BS // QUADS])
        rstd_sb = sq_sb
        eps_sb = sb("eps_sb", [P, 1])
        z_cat = sb("z_cat", [C, 2, BS])
        a1 = sb("a1", [P, M1, BS])
        a2 = a1[:, 0:M2, :]
        assert len(HOT) * HOT_CHUNKS * E <= M1 * BS
        hot_table = a1[0:HOT_ROWS, :, :].rearrange("p m (c e) -> p (m c) e", e=E)[
            :, 0:len(HOT) * HOT_CHUNKS, :]
        y_sb = h_sb[0:1, :]
        flats = [windows[0:64, FRONTS_FIRST:GROUPS, :].rearrange("p u b -> p (u b)"),
                 products[0:64, :, :, :].rearrange("p r u b -> p (r u b)")]
        staging = [flat[:, s * PIECE:(s + 1) * PIECE]
                   for flat, size in zip(flats, ((GROUPS - FRONTS_FIRST) * BS, RING * GROUP * BS))
                   for s in range(size // PIECE)]
        STAGES = len(staging)

        t_ps = ctx.enter_context(nc.psum_tensor("t_ps", [P, 2, GROUP, BS], F32))
        mover_ps = ctx.enter_context(nc.psum_tensor("mover_ps", [P, 2, BS], F32))
        window_ps = ctx.enter_context(nc.psum_tensor("window_ps", [P, 2 * BS], F32))
        h_ps = ctx.enter_context(nc.psum_tensor("h_ps", [P, 2 * BS], F32))
        mlp_ps = ctx.enter_context(nc.psum_tensor("mlp_ps", [P, 2, BS], F32))

        weights_in = [sem(f"weights_in{s}") for s in range(len(staging))]
        dense_in = sem("dense_in")
        params_in = sem("params_in")
        ids_in = [sem(f"ids_in{s}") for s in range(2)]
        hot_table_in = sem("hot_table_in")
        hot_ids_in = sem("hot_ids_in")
        hot_high = sem("hot_high")
        hot_low = sem("hot_low")
        hot_converted = sem("hot_converted")
        hot_squared = sem("hot_squared")
        hot_ready = sem("hot_ready")
        context_in = [sem(f"context_in{s}") for s in range(2)]
        gathered = [sem(f"gathered{g}") for g in range(GROUPS)]
        high_weights = sem("high_weights")
        low_weights = sem("low_weights")
        constants = sem("constants")
        identity_rounded = sem("identity_rounded")
        high_split = sem("high_split")
        low_split = sem("low_split")
        h_cleared = sem("h_cleared")
        movers_transposed = sem("movers_transposed")
        windows_transposed = sem("windows_transposed")
        movers_ready = sem("movers_ready")
        windows_ready = sem("windows_ready")
        t_ready = sem("t_ready")
        multiplied = sem("multiplied")
        contracted = sem("contracted")
        h_copied = sem("h_copied")
        mlp_mm = sem("mlp_mm")
        mlp_act = sem("mlp_act")
        normed = sem("normed")
        out_done = sem("out_done")

        block = ctx.enter_context(nc.Block())

        class Step:

            def __init__(self, k, half, parity, first=False, last=False):
                self.k, self.half, self.parity, self.first, self.last = k, half, parity, first, last

            def before(self):
                return Step(self.k - 1, self.half - (1 - self.parity), 1 - self.parity)

            def after(self):
                return Step(self.k + 1, self.half + self.parity, 1 - self.parity)

        def each_block(engine, emit):
            emit(Step(0, 0, 0, first=True))
            with engine.Fori(0, BLOCKS // 2 - 1) as i:
                emit(Step(2 * i + 1, i, 1))
                emit(Step(2 * i + 2, i + 1, 0))
            emit(Step(BLOCKS - 1, BLOCKS // 2 - 1, 1, last=True))

        def for_next(i, g):
            return g < TILES[i][0]

        def up_bank(c):
            return t_ps[:, c // 2, 2 * (c % 2), :]

        def movers_slot(b, g):
            return (GROUPS * b.parity + g) % MOVERS_RING

        def t_slot(b, i):
            return (NT * b.parity + i) % 2

        def pieces_before(g):
            return range(sum(PIECES_BEFORE[:g]), sum(PIECES_BEFORE[:g + 1]))

        ACT_STEPS = 8
        CONSTANTS = 5 + 2 * QUADS
        PARAMS = 14
        NORM_STEPS = 3

        @block.sync
        def _(sp):
            for piece in range(PIECES):
                s = piece % STAGES
                if piece >= STAGES:
                    sp.wait_ge(high_weights, piece - STAGES + 1)
                    sp.wait_ge(low_weights, piece - STAGES + 1)
                for copy in range(2):
                    sp.dma_start(staging[s][copy * E:(copy + 1) * E, :],
                                 w_units[:, piece * PIECE:(piece + 1) * PIECE]).then_inc(weights_in[s], 16)
                if piece == STAGES - 1:
                    sp.dma_start(hot_rows_sb[:, :], hot_rows).then_inc(hot_table_in, 16)
                    for h, f in enumerate(HOT):
                        sp.dma_start(hot_table[:, h * HOT_CHUNKS:(h + 1) * HOT_CHUNKS, :],
                                     tables[f].rearrange("(c p) e -> p c e", p=HOT_ROWS)
                                     ).then_inc(hot_table_in, 16)
                    for f in range(GROUP):
                        sp.dma_start(dw_sb[f * E:(f + 1) * E, :, :],
                                     dw[f:f + 1, :, :].broadcast_to([E, UNITS, D])).then_inc(dense_in, 16)
            sp.wait_ge(h_cleared, 2)
            for dst, src, quads in ((db_sb, dense_b, 1), (gamma_sb, gamma, QUADS), (beta_sb, beta, QUADS)):
                for q in range(quads):
                    sp.dma_start(dst[QUAD * q:QUAD * q + D, :], src.rearrange("(d o) -> d o", o=1)
                                 ).then_inc(params_in, 16)
            sp.dma_start(w1_sb[:, :], w1).then_inc(params_in, 16)
            sp.dma_start(w2_sb[:, :, :], w2.rearrange("(m p) n -> p m n", p=P)).then_inc(params_in, 16)
            sp.dma_start(w3_sb[:, :], w3).then_inc(params_in, 16)
            sp.dma_start(b1_sb[:, :], b1).then_inc(params_in, 16)
            sp.dma_start(b2_sb[:, :], b2).then_inc(params_in, 16)

        @block.gpsimd
        def _(pool):
            pool.memset(identity[:], 0.0).then_inc(constants, 1)
            pool.memset(centering[:], -1.0 / D).then_inc(constants, 1)
            pool.memset(averaging[:], 0.0).then_inc(constants, 1)
            pool.memset(eps_sb[:], LN_EPS).then_inc(constants, 1)
            to_be_read = [pool.alloc_register(f"to_be_read{s}") for s in range(2)]
            pool.reg_mov(to_be_read[0], 1)

            def finish_constants():
                pool.wait_ge(constants, 4)
                pool.affine_select(out=identity[:], in_=identity[:], compare_op=ALU.not_equal, fill=1.0,
                                   base=0, pattern=[[-1, P]], channel_multiplier=1).then_inc(constants, 1)
                for q in range(QUADS):
                    pool.wait_ge(constants, 5 + 2 * q)
                    pool.memset(averaging[QUAD * q:QUAD * q + D, QUAD * q:QUAD * (q + 1)], 1.0 / D
                                ).then_inc(constants, 1)
                    pool.wait_ge(constants, 6 + 2 * q)
                    pool.affine_select(out=centering[:], in_=centering[:], compare_op=ALU.not_equal,
                                       fill=1.0 - 1.0 / D, base=-QUAD * q, pattern=[[-1, QUAD]],
                                       channel_multiplier=1).then_inc(constants, 1)

            def gather(b, g):
                if g == 0:
                    pool.wait_ge(ids_in[b.parity], 16 * (b.half + 1))
                if not b.first:
                    count = GROUPS * (b.k - 1) + g + 1 if b.last else to_be_read[g % 2]
                    pool.wait_ge(low_split, count)
                    pool.wait_ge(windows_transposed, count)
                    if not b.last:
                        pool.reg_add(to_be_read[(g + 1) % 2], to_be_read[g % 2], 1)
                for t in range(BT):
                    for f in range(plain_fields(g)):
                        field = GROUP * g + f
                        pool.indirect_dma_start(
                            x_nat[:, g, t, f * E:(f + 1) * E], None, tables[field][:, :],
                            bass.IndirectOffsetOnAxis(ap=ids_sb[:, b.parity, t, field:field + 1], axis=0)
                        ).then_inc(gathered[g], 16)

            def emit(b):
                for g in range(GROUPS):
                    gather(b, g)

            finish_constants()
            each_block(pool, emit)

        @block.scalar
        def _(act):
            def load_ids(b):
                act.dma_start(ids_sb[:, b.parity, :, :],
                              ids[bass.ds(b.k * BS, BS), :].rearrange("(t p) f -> p t f", p=P)
                              ).then_inc(ids_in[b.parity], 16)

            def load_hot_ids(b, h):
                if not b.first or h > 0:
                    act.wait_ge(hot_squared, HOT_CHUNKS * (len(HOT) * b.k + h))
                act.dma_start(hot_ids_sb[:, :],
                              hot_ids[h:h + 1, bass.ds(b.k * BS, BS)].broadcast_to([HOT_ROWS, BS])
                              ).then_inc(hot_ids_in, 16)

            def make_one_hot(b, h, place):
                use = len(HOT) * b.k + h
                if place == 0:
                    act.wait_ge(hot_ids_in, 16 * (use + 1))
                    if h > 0:
                        act.wait_ge(windows_transposed, GROUPS * b.k + HOT_GROUPS[0] + 1)
                    elif not b.first:
                        act.wait_ge(windows_transposed, GROUPS * (b.k - 1) + HOT_GROUPS[1] + 1)
                    act.activation(hot_ids_f, hot_ids_sb[:, :], ACT.Copy).then_inc(hot_converted, 1)
                    act.wait_ge(hot_converted, use + 1)
                if place > 0:
                    act.wait_ge(hot_squared, HOT_CHUNKS * use + place)
                    last = act.activation(one_hot[:, place - 1, :], one_hot[:, place - 1, :].bitcast(F32),
                                          ACT.Relu, bias=1.0, scale=-1.0)
                if place < HOT_CHUNKS:
                    act.activation(one_hot[:, place, :], hot_ids_f, ACT.Square,
                                   bias=hot_rows_sb[:, place:place + 1]).then_inc(hot_squared, 1)
                else:
                    last.then_inc(hot_ready, 1)

            def load_context(b):
                act.dma_start(z_cat[D:C, b.parity, :], ctx_t[:, bass.ds(b.k * BS, BS)]
                              ).then_inc(context_in[b.parity], 16)

            load_ids(Step(0, 0, 0))
            load_hot_ids(Step(0, 0, 0, first=True), 0)

            def split_high(b, g):
                act.wait_ge(gathered[g], BT * plain_fields(g) * 16 * (b.k + 1))
                if not b.first or g >= XS_RING:
                    act.wait_ge(movers_transposed, GROUPS * b.k + g - XS_RING + 1)
                n = plain_fields(g)
                xs = x_split[:, g % XS_RING, :, 0:n, :, :]
                act.activation(xs[:, :, :, 0, :],
                               x_nat[:, g, :, 0:n * E].rearrange("p t (f e) -> p t f e", e=E),
                               ACT.Copy).then_inc(high_split, 1)

            def evacuate(b, g):
                seq = GROUPS * b.k + g
                act.wait_ge(movers_transposed, seq + 1)
                if not b.first or g >= MOVERS_RING:
                    behind = b if g >= MOVERS_RING else b.before()
                    act.wait_ge(t_ready, NT * behind.k + TILES_BEFORE[(g - MOVERS_RING) % GROUPS + 1])
                slot = movers[:, movers_slot(b, g), :, :].rearrange("p (a c) b -> p a c b", c=2)
                for odd in range(2):
                    for half in range(2):
                        last = act.activation(slot[half * 64:(half + 1) * 64, :, odd, :],
                                              mover_ps[odd * 64:(odd + 1) * 64, :, :], ACT.Copy)
                last.then_inc(movers_ready, 1)
                act.wait_ge(windows_transposed, seq + 1)
                if not b.first:
                    act.wait_ge(multiplied, NT * (b.k - 1) + TILES_BEFORE[GROUPS - 1] + g + 1)
                act.activation(windows[:, g, :], window_ps[:, 0:BS], ACT.Copy
                               ).then_inc(windows_ready, 1)

            def mlp(b, stage, final=False):
                stage_no = list(MLP_AFTER.values()).index(stage)
                act.wait_ge(mlp_mm, MLP_STAGES * b.k + stage_no + 1)
                done = ACT_STEPS * b.k
                if stage == "center":
                    act.activation(sq_sb[:, :], mlp_ps[:, 0, 0:BS // QUADS], ACT.Square
                                   ).then_inc(mlp_act, 1)
                elif stage == "variance":
                    act.activation(std_sb[:, :], mlp_ps[:, 1, 0:BS // QUADS], ACT.Sqrt, bias=eps_sb[:, :]
                                   ).then_inc(mlp_act, 1)
                elif stage.startswith("up") and final:
                    c = int(stage[-1])
                    act.activation(a1[:, c, :], up_bank(c), ACT.Relu, bias=b1_sb[:, c:c + 1]
                                   ).then_inc(mlp_act, 1)
                elif stage in ("up_1", "up_3"):
                    for m in range(2):
                        c = int(stage[-1]) - 1 + m
                        act.activation(a1[:, c, :], mlp_ps[:, m, :], ACT.Relu, bias=b1_sb[:, c:c + 1]
                                       ).then_inc(mlp_act, 1)
                elif stage == "middle_7":
                    for m in range(2):
                        last = act.activation(a2[:, m, :], mlp_ps[:, m, :], ACT.Relu,
                                              bias=b2_sb[:, m:m + 1])
                    last.then_inc(mlp_act, 1)
                elif stage == "out":
                    act.activation(y_sb[:, :], mlp_ps[0:1, 0, :], ACT.Copy).then_inc(mlp_act, 1)
                    act.wait_ge(mlp_act, done + ACT_STEPS)
                    act.dma_start(out[bass.ds(b.k * BS, BS), :].rearrange("b o -> o b"), y_sb[:, :]
                                  ).then_inc(out_done, 16)

            def copy_h(b):
                act.wait_ge(params_in, PARAMS * 16)
                act.wait_ge(contracted, NT * (b.k + 1))
                act.activation(h_sb[:, :], h_ps[:, 0:BS], ACT.Identity,
                               bias=db_sb[:, :]).then_inc(h_copied, 1)

            def split_weights_high(pieces):
                for piece in pieces:
                    s = piece % STAGES
                    act.wait_ge(weights_in[s], 32 * (piece // STAGES + 1))
                    act.activation(w_split[0:64, piece * PIECE:(piece + 1) * PIECE], staging[s], ACT.Copy
                                   ).then_inc(high_weights, 1)

            split_weights_high(pieces_before(0)[:PIECES_ALONE])
            act.wait_ge(hot_table_in, 16 * (1 + len(HOT)))
            act.activation(hot_split[:, :, 0, :], hot_table[:, :, :], ACT.Copy).then_inc(hot_high, 1)
            act.activation(hot_flat[:, 0:HOT_LEAD], a1[0:HOT_ROWS, 0, 0:HOT_LEAD], ACT.Copy
                           ).then_inc(hot_high, 1)
            for place in range(HOT_CHUNKS + 1):
                make_one_hot(Step(0, 0, 0, first=True), 0, place)
                split_weights_high(pieces_before(0)[PIECES_ALONE + place:PIECES_ALONE + place + 1])
            act.wait_ge(constants, CONSTANTS)
            act.activation(identity_r[:, :], identity[:, :], ACT.Copy).then_inc(identity_rounded, 1)
            for g in range(len(PIECES_BEFORE)):
                split_high(Step(0, 0, 0, first=True), g)
                split_weights_high(pieces_before(g + 1)[:HIGH_FIRST])
                if g < FRONTS_FIRST:
                    evacuate(Step(0, 0, 0, first=True), g)
                split_weights_high(pieces_before(g + 1)[HIGH_FIRST:])

            def emit(b):
                if not b.last:
                    load_ids(b.after())
                load_context(b)
                for i in range(NT):
                    if i == HOT_LOAD_AFTER[1]:
                        load_hot_ids(b, 1)
                    if i == HOT_LOAD_AFTER[0] and not b.last:
                        load_hot_ids(b.after(), 0)
                    if i - HOT_AFTER[1] in range(HOT_CHUNKS + 1):
                        make_one_hot(b, 1, i - HOT_AFTER[1])
                    if i - HOT_AFTER[0] in range(HOT_CHUNKS + 1) and not b.last:
                        make_one_hot(b.after(), 0, i - HOT_AFTER[0])
                    if i == COPY_H_AFTER and not b.first:
                        copy_h(b.before())
                    if i in MLP_AFTER and not b.first:
                        mlp(b.before(), MLP_AFTER[i])
                    if i == STORED_AFTER and not b.first:
                        act.wait_ge(out_done, 16 * b.k)
                    for events, do in ((SPLIT_AFTER, split_high), (FRONT_AFTER, evacuate)):
                        if i in events and not (b.last and for_next(i, events[i])):
                            do(b.after() if for_next(i, events[i]) else b, events[i])

            each_block(act, emit)
            final = Step(BLOCKS - 1, BLOCKS // 2 - 1, 1)
            copy_h(final)
            for stage in MLP_AFTER.values():
                mlp(final, stage, final=True)
            act.wait_ge(out_done, 16 * BLOCKS)

        @block.vector
        def _(dve):
            dve.memset(h_ps[:, :], 0.0).then_inc(h_cleared, 1)
            dve.memset(db_sb[:, :], 0.0).then_inc(h_cleared, 1)

            def split_low(b, g):
                dve.wait_ge(high_split, GROUPS * b.k + g + 1)
                dve.wait_ge(gathered[g], BT * plain_fields(g) * 16 * (b.k + 1))
                n = plain_fields(g)
                xs = x_split[:, g % XS_RING, :, 0:n, :, :]
                dve.tensor_tensor(xs[:, :, :, 1, :],
                                  x_nat[:, g, :, 0:n * E].rearrange("p t (f e) -> p t f e", e=E),
                                  xs[:, :, :, 0, :].bitcast(F32), ALU.subtract).then_inc(low_split, 1)

            def split_hot_low():
                dve.wait_ge(hot_table_in, 16 * (1 + len(HOT)))
                dve.wait_ge(hot_high, 1)
                dve.tensor_tensor(hot_split[:, :, 1, :], hot_table[:, :, :],
                                  hot_split[:, :, 0, :].bitcast(F32), ALU.subtract).then_inc(hot_low, 1)

            def split_weights_low(pieces):
                for piece in pieces:
                    s = piece % STAGES
                    dve.wait_ge(weights_in[s], 32 * (piece // STAGES + 1))
                    dve.wait_ge(high_weights, piece + 1)
                    at = slice(piece * PIECE, (piece + 1) * PIECE)
                    dve.tensor_tensor(w_split[64:P, at], staging[s], w_split[0:64, at].bitcast(F32),
                                      ALU.subtract).then_inc(low_weights, 1)

            def multiply(b, i):
                n = NT * b.k + i
                g, w = TILES[i]
                dve.wait_ge(t_ready, n + 1)
                if w == 0:
                    dve.wait_ge(windows_ready, GROUPS * b.k + g + 1)
                if not b.first or i >= RING:
                    dve.wait_ge(contracted, n + 1 - RING)
                count = UNITS_IN[i]
                window = windows[:, w, :].unsqueeze(1).broadcast_to([P, count, BS])
                dve.tensor_tensor(products[:, i % RING, 0:count, :], t_ps[:, t_slot(b, i), 0:count, :],
                                  window, ALU.mult).then_inc(multiplied, 1)

            def norm(b):
                dve.wait_ge(params_in, PARAMS * 16)
                dve.wait_ge(mlp_act, ACT_STEPS * b.k + 2)
                dve.reciprocal(rstd_sb[:, :], std_sb[:, :]).then_inc(normed, 1)
                dve.wait_ge(normed, NORM_STEPS * b.k + 1)
                dve.tensor_tensor(rstd_sb[:, :], mlp_ps[:, 0, 0:BS // QUADS], rstd_sb[:, :],
                                  ALU.mult).then_inc(normed, 1)
                dve.wait_ge(normed, NORM_STEPS * b.k + 2)
                for q in range(QUADS):
                    rows = slice(QUAD * q, QUAD * q + D)
                    last = dve.tensor_scalar(z_cat[0:D, b.parity, q * BS // QUADS:(q + 1) * BS // QUADS],
                                             rstd_sb[rows, :], gamma_sb[rows, :], beta_sb[rows, :],
                                             ALU.mult, ALU.add)
                last.then_inc(normed, 1)

            for g in range(len(PIECES_BEFORE)):
                split_weights_low(pieces_before(g))
                if g == 0:
                    split_hot_low()
                split_low(Step(0, 0, 0, first=True), g)

            def emit(b):
                for i in range(NT):
                    multiply(b, i)
                    if i == MLP_NORM_AFTER and not b.first:
                        norm(b.before())
                    if i in SPLIT_AFTER and not (b.last and for_next(i, SPLIT_AFTER[i])):
                        split_low(b.after() if for_next(i, SPLIT_AFTER[i]) else b, SPLIT_AFTER[i])

            each_block(dve, emit)
            norm(Step(BLOCKS - 1, BLOCKS // 2 - 1, 1))

        @block.tensor
        def _(pe):
            def hot_columns(c, half, count):
                end = HOT_LEAD + (2 * c + half) * E + count
                return hot_flat[:, end - P:end]

            def gather_hot(b, h, part):
                seq = GROUPS * b.k + HOT_GROUPS[h]
                if part == 0:
                    pe.wait_ge(hot_ready, len(HOT) * b.k + h + 1)
                    if not b.first or h > 0:
                        pe.wait_ge(movers_ready, seq)
                        pe.wait_ge(windows_ready, seq)
                for n in range(part * HOT_CHUNKS // HOT_PARTS, (part + 1) * HOT_CHUNKS // HOT_PARTS):
                    c = h * HOT_CHUNKS + n
                    pe.matmul(mover_ps[:, 1, :], hot_columns(c, 0, 2 * E), one_hot[:, n, :],
                              start=(n == 0), stop=(n == HOT_CHUNKS - 1))
                    for half in range(2):
                        pe.matmul(window_ps[:, 0:BS], hot_columns(c, half, E), one_hot[:, n, :],
                                  start=(n + half == 0), stop=(n == HOT_CHUNKS - 1 and half == 1))

            def transpose_group(b, g):
                seq = GROUPS * b.k + g
                pe.wait_ge(low_split, seq + 1)
                if not b.first or g >= 1:
                    pe.wait_ge(movers_ready, seq)
                for pair in range(2):
                    fields = 1 if g in HOT_GROUPS and pair == 1 else 2
                    for t in range(BT):
                        last = pe.matmul(
                            mover_ps[0:fields * 2 * E, pair, t * P:(t + 1) * P],
                            x_split[:, g % XS_RING, t, 2 * pair:2 * pair + fields, :, :].rearrange(
                                "p f h e -> p (f h e)"),
                            identity_r[:, :], start=True, stop=True)
                last.then_inc(movers_transposed, 1)
                if not b.first or g >= 1:
                    pe.wait_ge(windows_ready, seq)
                pe.wait_ge(gathered[g], BT * plain_fields(g) * 16 * (b.k + 1))
                rows = plain_fields(g) * E
                for t in range(BT):
                    last = pe.transpose(window_ps[0:rows, t * P:(t + 1) * P], x_nat[:, g, t, 0:rows],
                                        identity[:, :])
                last.then_inc(windows_transposed, 1)

            def interact(b, i):
                n = NT * b.k + i
                g, w = TILES[i]
                if w == 0:
                    pe.wait_ge(movers_ready, GROUPS * b.k + g + 1)
                if not b.first or n >= 2:
                    pe.wait_ge(multiplied, n - 1)
                for at, j in enumerate(TILE_MOVERS[i]):
                    u = UNITS_BEFORE[i] + at
                    last = pe.matmul(t_ps[:, t_slot(b, i), at, :], w_split[:, u * P:(u + 1) * P],
                                     movers[:, movers_slot(b, g), j % GROUP, :], start=True, stop=True)
                last.then_inc(t_ready, 1)

            def contract(b, i):
                pe.wait_ge(multiplied, NT * b.k + i + 1)
                if i == 0 and not b.first:
                    pe.wait_ge(h_copied, b.k)
                for at in range(UNITS_IN[i]):
                    u = UNITS_BEFORE[i] + at
                    q = u % QUADS
                    last = pe.matmul(h_ps[QUAD * q:QUAD * q + D, 0:BS], dw_sb[:, u, :],
                                     products[:, i % RING, at, :], start=(u < QUADS), stop=(u >= UNITS - QUADS))
                last.then_inc(contracted, 1)

            def mlp(b, stage, final=False):
                done = ACT_STEPS * b.k
                if stage == "center":
                    pe.wait_ge(params_in, PARAMS * 16)
                    pe.wait_ge(h_copied, b.k + 1)
                    for q in range(QUADS):
                        last = pe.matmul(mlp_ps[QUAD * q:QUAD * (q + 1), 0, 0:BS // QUADS], centering[:, :],
                                         h_sb[:, q * BS // QUADS:(q + 1) * BS // QUADS],
                                         start=True, stop=True)
                elif stage == "variance":
                    pe.wait_ge(mlp_act, done + 1)
                    last = pe.matmul(mlp_ps[:, 1, 0:BS // QUADS], averaging[:, :], sq_sb[:, :],
                                     start=True, stop=True)
                elif stage.startswith("up"):
                    c = int(stage[-1])
                    out_ps = up_bank(c) if final else mlp_ps[:, c % 2, :]
                    if c == 0:
                        pe.wait_ge(normed, NORM_STEPS * (b.k + 1))
                        pe.wait_ge(context_in[b.parity], 16 * (b.half + 1))
                    elif c == 2 and not final:
                        pe.wait_ge(mlp_act, done + 4)
                    last = pe.matmul(out_ps, w1_sb[:, c * P:(c + 1) * P], z_cat[:, b.parity, :],
                                     start=True, stop=True)
                elif stage != "out":
                    m, c = divmod(int(stage[-1]), M1)
                    if m == 0 and (c == 0 or final):
                        pe.wait_ge(mlp_act, done + (3 + c if final else 6))
                    last = pe.matmul(mlp_ps[:, m, :], w2_sb[:, c, m * P:(m + 1) * P], a1[:, c, :],
                                     start=(c == 0), stop=(c == M1 - 1))
                else:
                    pe.wait_ge(mlp_act, done + 7)
                    for c in range(M2):
                        last = pe.matmul(mlp_ps[0:1, 0, :], w3_sb[:, c:c + 1], a2[:, c, :],
                                         start=(c == 0), stop=(c == M2 - 1))
                last.then_inc(mlp_mm, 1)

            pe.wait_ge(constants, CONSTANTS)
            pe.wait_ge(identity_rounded, 1)
            pe.wait_ge(hot_low, 1)
            pe.wait_ge(hot_high, 2)
            for part in range(HOT_PARTS):
                gather_hot(Step(0, 0, 0, first=True), 0, part)
            for g in range(FRONTS_FIRST):
                transpose_group(Step(0, 0, 0, first=True), g)
            pe.wait_ge(low_weights, PIECES)
            pe.wait_ge(high_weights, PIECES)
            pe.wait_ge(dense_in, 16 * GROUP)
            pe.wait_ge(h_cleared, 1)

            def emit(b):
                for i in range(NT):
                    stage = None if b.first else MLP_AFTER.get(i)
                    if stage:
                        mlp(b.before(), stage)
                    if i >= CONTRACT_LAG:
                        contract(b, i - CONTRACT_LAG)
                    elif not b.first:
                        contract(b.before(), NT + i - CONTRACT_LAG)
                    interact(b, i)
                    if i in HOT_PARTS_AFTER[1]:
                        gather_hot(b, 1, HOT_PARTS_AFTER[1].index(i))
                    if i in HOT_PARTS_AFTER[0] and not b.last:
                        gather_hot(b.after(), 0, HOT_PARTS_AFTER[0].index(i))
                    if i in FRONT_AFTER and not (b.last and for_next(i, FRONT_AFTER[i])):
                        transpose_group(b.after() if for_next(i, FRONT_AFTER[i]) else b, FRONT_AFTER[i])

            each_block(pe, emit)
            final = Step(BLOCKS - 1, BLOCKS // 2 - 1, 1)
            for i in range(NT - CONTRACT_LAG, NT):
                contract(final, i)
            for stage in MLP_AFTER.values():
                mlp(final, stage, final=True)


def layouts(w, dense_w):
    import numpy as np

    pair = {}
    for i in range(FIELDS):
        for j in range(i + 1, FIELDS):
            pair[i, j] = len(pair)
    w_units = np.zeros((E, UNITS, P), w.dtype)
    dw = np.zeros((GROUP, UNITS, D), dense_w.dtype)
    order = [(j, window) for (_, window), movers in zip(TILES, TILE_MOVERS) for j in movers]
    for u, (j, window) in enumerate(order):
        for s in range(GROUP):
            i = GROUP * window + s
            if i < j:
                w_units[:, u, s * E:(s + 1) * E] = w[pair[i, j]].T
                dw[s, u] = dense_w[pair[i, j]]
    return w_units.reshape(E, UNITS * P), dw


def by_partition(v):
    import numpy as np

    return np.asarray(v).reshape(-1, P).T


def kernel(**inputs):
    import numpy as np
    import concourse.bacc as bacc
    from concourse.bass_utils import run_bass_kernel_spmd

    w_units, dw = layouts(np.asarray(inputs["L0_rec_W"]), np.asarray(inputs["L0_rec_dense_w"]))
    rows = -np.arange(inputs[f"tbl_{HOT[0]}"].shape[0], dtype=np.float32)
    arrays = {"ids": inputs["ids"], "hot_ids": np.asarray(inputs["ids"])[:, HOT].T,
              "hot_rows": rows.reshape(HOT_CHUNKS, -1).T}
    for f in range(FIELDS):
        arrays[f"tbl_{f}"] = inputs[f"tbl_{f}"]
    arrays.update(
        w_units=w_units, dw=dw,
        dense_b=inputs["L0_rec_dense_b"], gamma=inputs["L0_rec_gamma"], beta=inputs["L0_rec_beta"],
        ctx_t=np.asarray(inputs["dense_ctx"]).T, w1=inputs["W_top1"], b1=by_partition(inputs["b_top1"]),
        w2=inputs["W_top2"], b2=by_partition(inputs["b_top2"]), w3=by_partition(inputs["W_top3"]))
    arrays = {name: np.ascontiguousarray(a) for name, a in arrays.items()}
    nc = bacc.Bacc("TRN2", target_bir_lowering=False, num_devices=1)
    aps = {name: nc.dram_tensor(f"in_{name}", a.shape, mybir.dt.from_np(a.dtype), kind="ExternalInput").ap()
           for name, a in arrays.items()}
    out = nc.dram_tensor("out", (arrays["ids"].shape[0], 1), F32, kind="ExternalOutput").ap()
    tables = [aps.pop(f"tbl_{f}") for f in range(FIELDS)]
    interaction_tower(nc, tables=tables, out=out, **aps)
    result = run_bass_kernel_spmd(nc, [{f"in_{name}": a for name, a in arrays.items()}], core_ids=[0])
    return result.results[0]["out"]
```
